# Optimizing a Trainium2 kernel written in Bass

```python
import numpy as np
import jax
import jax.numpy as jnp

def _softmax(x, axis=-1):
    return jax.nn.softmax(x, axis=axis)

def _gelu(x):
    return jax.nn.gelu(x, approximate=True)

def _silu(x):
    return jax.nn.silu(x)

def _sigmoid(x):
    return jax.nn.sigmoid(x)

def _layernorm(x, axis=-1, eps=1e-05):
    m = jnp.mean(x, axis=axis, keepdims=True)
    v = jnp.var(x, axis=axis, keepdims=True)
    return (x - m) / jnp.sqrt(v + eps)

def _scatter_add(tgt, idx, src, axis=0):
    return tgt.at[idx].add(src)

def _segment_sum(src, seg, n):
    return jax.ops.segment_sum(src, seg, n)
kernel_name = 'mk_flamingo_gated_d2_seqx_r8_ec521e'

def setup_inputs(seed: int=0):
    np.random.seed(seed)
    _w = jnp.asarray

    def _rec_inputs():
        import jax
        import jax.numpy as jnp
        _rk = jax.random.key(seed)
        x = -0.0002928 + 1 * jax.random.normal(jax.random.fold_in(_rk, 1), (8, 128, 256), jnp.float32)
        _lenS = 128 - jax.random.randint(jax.random.fold_in(_rk, 7), (8,), 0, max(1, 128 // 4) + 1, jnp.int32)
        _lenS2 = 128 - jax.random.randint(jax.random.fold_in(_rk, 8), (8,), 0, max(1, 128 // 4) + 1, jnp.int32)
        fside_S2_0 = -0.00337071 + 1.01897 * jax.random.normal(jax.random.fold_in(_rk, 11), (128,), jnp.float32)
        _ctx_2048P = jax.random.normal(jax.random.fold_in(_rk, 12), (8, 16, 256), jnp.float32)
        _ctx_2048c = jax.random.dirichlet(jax.random.fold_in(_rk, 512), 0.3 * jnp.ones((16,), jnp.float32), (8, 128))
        _ctx_2048t = jnp.einsum('bsk,bkd->bsd', _ctx_2048c, _ctx_2048P)
        _ctx_2048t = _ctx_2048t * jax.lax.rsqrt(jnp.mean(jnp.square(_ctx_2048t)) + 1e-12) * 0.953939
        ctx_2048 = 0.000675642 + 1.00031 * (_ctx_2048t + 0.3 * jax.random.normal(jax.random.fold_in(_rk, 612), (8, 128, 256), jnp.float32))
        _g = jax.random.normal(jax.random.fold_in(_rk, 9001), (2, 2), jnp.float32)
        _g = jnp.sign(_g) * jnp.maximum(jnp.abs(_g), 1.0) + (_g == 0) * 1.0
        g_xattn = _g[0]
        g_ffn = _g[1]
        return (x, fside_S2_0, ctx_2048, g_xattn, g_ffn)
    x, fside_S2_0, ctx_2048, g_xattn, g_ffn = _rec_inputs()

    def _L0_xattn_setup():
        import jax, jax.numpy as jnp
        import numpy as np
        key = jax.random.key(seed)
        ks = jax.random.split(key, 5)
        B, D, L, NH = (2, 128, 256, 8)
        H = D // NH
        return {'v': jax.random.normal(ks[0], (B, D, L), jnp.float32), 'k': jax.random.normal(ks[1], (H, L), jnp.float32) * 0.1, 'bias': jax.random.normal(ks[2], (D,), jnp.float32), 'x1': jax.random.normal(ks[3], (B, D, L), jnp.float32), 'x2': jax.random.normal(ks[4], (B, D, L), jnp.float32), 'num_heads': NH}
    _L0_xattn_all = _L0_xattn_setup()
    _L0_xattn_in = {k: v for k, v in _L0_xattn_all.items() if k in ('k',)}
    del _L0_xattn_all

    def _L0_ffn_setup():
        import jax, jax.numpy as jnp
        import numpy as np
        SEQ, BS, D, F, E = (128, 2, 256, 256, 8)
        key = jax.random.key(seed)
        ks = jax.random.split(key, 8)
        s = 0.02
        return {'hidden_states': jax.random.normal(ks[0], (SEQ, BS, D), jnp.float32), 'router_w': jax.random.normal(ks[1], (D, E), jnp.float32) * s, 'gate_w': jax.random.normal(ks[2], (E, D, F), jnp.float32) * s, 'up_w': jax.random.normal(ks[3], (E, D, F), jnp.float32) * s, 'down_w': jax.random.normal(ks[4], (E, F, D), jnp.float32) * s, 'shared_gate_w': jax.random.normal(ks[5], (D, F), jnp.float32) * s, 'shared_up_w': jax.random.normal(ks[6], (D, F), jnp.float32) * s, 'shared_down_w': jax.random.normal(ks[7], (F, D), jnp.float32) * s}
    _L0_ffn_all = _L0_ffn_setup()
    _L0_ffn_in = {k: v for k, v in _L0_ffn_all.items() if k in ('router_w', 'gate_w', 'up_w', 'down_w', 'shared_gate_w', 'shared_up_w', 'shared_down_w')}
    del _L0_ffn_all

    def _L1_xattn_setup():
        import jax, jax.numpy as jnp
        import numpy as np
        key = jax.random.key(seed)
        k1, k2, k3, k4, k5 = jax.random.split(key, 5)
        B, D_MODEL, L = (2, 128, 256)
        HEAD_DIM = 8
        H = D_MODEL // HEAD_DIM
        return {'k': jax.random.normal(k1, (B, D_MODEL, L), dtype=jnp.float32), 'v': jax.random.normal(k2, (B, D_MODEL, L), dtype=jnp.float32), 'q': jax.random.normal(k3, (B, D_MODEL, L), dtype=jnp.float32), 'ssm_kernel': jax.random.normal(k4, (H, L), dtype=jnp.float32), 'D': jax.random.normal(k5, (H,), dtype=jnp.float32), 'head_dim': HEAD_DIM}
    _L1_xattn_all = _L1_xattn_setup()
    _L1_xattn_in = {k: v for k, v in _L1_xattn_all.items() if k in ('ssm_kernel', 'D')}
    del _L1_xattn_all

    def _L1_ffn_setup():
        import jax, jax.numpy as jnp
        import numpy as np
        H = 256
        E = 64
        I = 64
        SI = 64
        TOP_K = 8
        B, T = (2, 64)
        key = jax.random.key(seed)
        ks = jax.random.split(key, 8)
        s = 0.02
        return {'h': jax.random.normal(ks[0], (B, T, H), jnp.float32), 'gate_w': jax.random.normal(ks[1], (E, H), jnp.float32) * s, 'gu_w': jax.random.normal(ks[2], (E, 2 * I, H), jnp.float32) * s, 'dp_w': jax.random.normal(ks[3], (E, H, I), jnp.float32) * s, 'sh_gate_w': jax.random.normal(ks[4], (SI, H), jnp.float32) * s, 'sh_up_w': jax.random.normal(ks[5], (SI, H), jnp.float32) * s, 'sh_down_w': jax.random.normal(ks[6], (H, SI), jnp.float32) * s, 'sh_gate1_w': jax.random.normal(ks[7], (1, H), jnp.float32) * s}
    _L1_ffn_all = _L1_ffn_setup()
    _L1_ffn_in = {k: v for k, v in _L1_ffn_all.items() if k in ('gate_w', 'gu_w', 'dp_w', 'sh_gate_w', 'sh_up_w', 'sh_down_w', 'sh_gate1_w')}
    del _L1_ffn_all
    return {'x': x, 'fside_S2_0': fside_S2_0, 'ctx_2048': ctx_2048, 'g_xattn': g_xattn, 'g_ffn': g_ffn, 'L0_xattn_k': _L0_xattn_in['k'], 'L0_ffn_router_w': _L0_ffn_in['router_w'], 'L0_ffn_gate_w': _L0_ffn_in['gate_w'], 'L0_ffn_up_w': _L0_ffn_in['up_w'], 'L0_ffn_down_w': _L0_ffn_in['down_w'], 'L0_ffn_shared_gate_w': _L0_ffn_in['shared_gate_w'], 'L0_ffn_shared_up_w': _L0_ffn_in['shared_up_w'], 'L0_ffn_shared_down_w': _L0_ffn_in['shared_down_w'], 'L1_xattn_ssm_kernel': _L1_xattn_in['ssm_kernel'], 'L1_xattn_D': _L1_xattn_in['D'], 'L1_ffn_gate_w': _L1_ffn_in['gate_w'], 'L1_ffn_gu_w': _L1_ffn_in['gu_w'], 'L1_ffn_dp_w': _L1_ffn_in['dp_w'], 'L1_ffn_sh_gate_w': _L1_ffn_in['sh_gate_w'], 'L1_ffn_sh_up_w': _L1_ffn_in['sh_up_w'], 'L1_ffn_sh_down_w': _L1_ffn_in['sh_down_w'], 'L1_ffn_sh_gate1_w': _L1_ffn_in['sh_gate1_w']}

def reference(x, fside_S2_0, ctx_2048, g_xattn, g_ffn, L0_xattn_k, L0_ffn_router_w, L0_ffn_gate_w, L0_ffn_up_w, L0_ffn_down_w, L0_ffn_shared_gate_w, L0_ffn_shared_up_w, L0_ffn_shared_down_w, L1_xattn_ssm_kernel, L1_xattn_D, L1_ffn_gate_w, L1_ffn_gu_w, L1_ffn_dp_w, L1_ffn_sh_gate_w, L1_ffn_sh_up_w, L1_ffn_sh_down_w, L1_ffn_sh_gate1_w):
    import jax
    import jax.numpy as jnp

    def _L0_xattn_ref(v, k, bias, x1, x2, num_heads):
        import jax, jax.numpy as jnp
        import numpy as np
        B, D, L = v.shape
        H = D // num_heads
        fft_size = 2 * L
        vr = v.reshape(B, H, num_heads, L)
        x1r = x1.reshape(B, H, num_heads, L)
        x2r = x2.reshape(B, H, num_heads, L)
        kv = vr[:, :, :, None, :] * x2r[:, :, None, :, :]
        k_f = jnp.fft.rfft(k.astype(jnp.float32), n=fft_size)
        y = jnp.fft.irfft(jnp.fft.rfft(kv, n=fft_size) * k_f[None, :, None, None, :], n=fft_size)[..., :L]
        skip = bias.astype(jnp.float32).reshape(H, num_heads)[None, :, :, None, None]
        y = y + kv * skip
        out = jnp.einsum('bhijl,bhil->bhjl', y, x1r)
        return out.reshape(B, D, L)

    def _L0_ffn_ref(hidden_states, router_w, gate_w, up_w, down_w, shared_gate_w, shared_up_w, shared_down_w):
        import jax, jax.numpy as jnp
        import numpy as np
        SEQ, BS, D, F, E = (128, 2, 256, 256, 8)
        S, B, Dm = hidden_states.shape
        x = hidden_states.reshape(-1, Dm)
        logits = x @ router_w
        expert_idx = jnp.argmax(logits, axis=-1)
        score = jax.nn.sigmoid(jnp.max(logits, axis=-1))
        xs = x * score[:, None]
        n_experts = router_w.shape[1]
        out = jnp.zeros_like(x)
        for e in range(n_experts):
            m = (expert_idx == e)[:, None]
            xe = jnp.where(m, xs, 0.0)
            h = jax.nn.silu(xe @ gate_w[e]) * (xe @ up_w[e])
            out = out + jnp.where(m, h @ down_w[e], 0.0)
        shared = jax.nn.silu(x @ shared_gate_w) * (x @ shared_up_w) @ shared_down_w
        return (out + shared).reshape(S, B, Dm)

    def _L1_xattn_ref(k, v, q, ssm_kernel, D, head_dim):
        import jax, jax.numpy as jnp
        import numpy as np
        B, HD, L = k.shape
        H = HD // head_dim
        fft_size = 2 * L
        k_ = k.reshape(B, H, head_dim, L)
        v_ = v.reshape(B, H, head_dim, L)
        q_ = q.reshape(B, H, head_dim, L)
        kv = jnp.einsum('bhil,bhjl->bijhl', k_, v_)
        kv_f = jnp.fft.rfft(kv, n=fft_size)
        kernel_f = jnp.fft.rfft(ssm_kernel, n=fft_size)
        y = jnp.fft.irfft(kv_f * kernel_f, n=fft_size)[..., :L]
        out = y + kv * D[None, None, None, :, None]
        out = jnp.einsum('bijhl,bhil->bjhl', out, q_)
        out = jnp.transpose(out, (0, 2, 1, 3)).reshape(B, H * head_dim, L)
        return out.astype(k.dtype)

    def _L1_ffn_ref(h, gate_w, gu_w, dp_w, sh_gate_w, sh_up_w, sh_down_w, sh_gate1_w):
        import jax, jax.numpy as jnp
        import numpy as np
        H = 256
        E = 64
        I = 64
        SI = 64
        TOP_K = 8
        B, T = (2, 64)
        Bb, Tt, Hh = h.shape
        x = h.reshape(Bb * Tt, Hh)
        N = x.shape[0]
        logits = x @ gate_w.T
        topv, topi = jax.lax.top_k(logits, TOP_K)
        rw = jax.nn.softmax(topv.astype(jnp.float32), axis=-1).astype(x.dtype)
        W = jnp.zeros((N, E), x.dtype).at[jnp.arange(N)[:, None], topi].set(rw)
        gu = jnp.einsum('nh,eih->nei', x, gu_w)
        gate, up = (gu[..., :I], gu[..., I:])
        inter = jax.nn.silu(gate) * up
        inter_w = inter * W[:, :, None]
        out = jnp.einsum('nei,ehi->nh', inter_w, dp_w)
        sh_inter = jax.nn.silu(x @ sh_gate_w.T) * (x @ sh_up_w.T)
        sh_out = sh_inter @ sh_down_w.T
        sh_g = jax.nn.sigmoid(x @ sh_gate1_w.T)
        out = out + sh_g * sh_out
        return out.reshape(Bb, Tt, Hh)
    x = x + jnp.tanh(g_xattn[0]) * _L0_xattn_ref(_layernorm(x, axis=-1), L0_xattn_k, fside_S2_0, ctx_2048, ctx_2048, 8)
    x = x + jnp.tanh(g_ffn[0]) * _L0_ffn_ref(_layernorm(x, axis=-1), L0_ffn_router_w, L0_ffn_gate_w, L0_ffn_up_w, L0_ffn_down_w, L0_ffn_shared_gate_w, L0_ffn_shared_up_w, L0_ffn_shared_down_w)
    x = x + jnp.tanh(g_xattn[1]) * _L1_xattn_ref(ctx_2048, ctx_2048, _layernorm(x, axis=-1), L1_xattn_ssm_kernel, L1_xattn_D, 8)
    x = x + jnp.tanh(g_ffn[1]) * _L1_ffn_ref(_layernorm(x, axis=-1), L1_ffn_gate_w, L1_ffn_gu_w, L1_ffn_dp_w, L1_ffn_sh_gate_w, L1_ffn_sh_up_w, L1_ffn_sh_down_w, L1_ffn_sh_gate1_w)
    return x

_drawn_inputs = setup_inputs


def setup_inputs(seed=0):
    import zlib

    import numpy as np

    out = dict(_drawn_inputs(seed))
    spreads = {'g_ffn': (-1.0, 0.6)}
    factors = {'L0_ffn_router_w': 8.0,
     'L0_ffn_gate_w': 8.0,
     'L0_ffn_up_w': 8.0,
     'L0_ffn_down_w': 8.0,
     'L0_ffn_shared_gate_w': 8.0,
     'L0_ffn_shared_up_w': 8.0,
     'L0_ffn_shared_down_w': 8.0,
     'L1_ffn_gate_w': 8.0,
     'L1_ffn_gu_w': 8.0,
     'L1_ffn_dp_w': 8.0,
     'L1_ffn_sh_gate_w': 8.0,
     'L1_ffn_sh_up_w': 8.0,
     'L1_ffn_sh_down_w': 8.0,
     'L1_ffn_sh_gate1_w': 8.0}
    for name, (base, spread) in spreads.items():
        noise = np.random.default_rng([zlib.crc32(name.encode()), seed]).standard_normal(out[name].shape)
        drawn = base * np.exp(spread * noise) if base else spread * noise
        out[name] = jnp.asarray(drawn.astype(out[name].dtype))
    for name, factor in factors.items():
        out[name] = (out[name] * factor).astype(out[name].dtype)
    return out
```

```python
from contextlib import ExitStack

import concourse.bass as bass
from concourse import mybir

P = 128
B, C, L = 8, 128, 256
LT = L // P
HEAD = 8
H = C // HEAD
PAIRS = HEAD * HEAD
PAD = P - 1
KP = 384
E0, F0 = 8, 256
BLOCKS = B * C // P + E0 - 1
SLOTS = BLOCKS * P
E1, I1 = 64, 64
NP1 = E1 // 2
R1 = E1 + 1
GROUP = 4
TOK = B * C
NT = TOK // 512
WCOLS = LT * 2 * P + L
WPARTS = (slice(0, LT * 2 * P), slice(LT * 2 * P, WCOLS))
EPS = 1e-5

F32 = mybir.dt.float32
F32R = mybir.dt.float32r
BF16 = mybir.dt.bfloat16
I32 = mybir.dt.int32
ALU = mybir.AluOpType
ACT = mybir.ActivationFunctionType
AX = mybir.AxisListType

K_ID, K_LESS, K_HEAD = 0, P, 2 * P
K_FIRST = 3 * P
K_FULL = K_FIRST + E0
K_UPTO = K_FULL + E0 * E0
K_BLOCK = K_UPTO + E0 * E0
K_COLS = K_BLOCK + E0 * BLOCKS


def shape_constants():
    import numpy as np
    k = np.zeros((P, K_COLS), np.float32)
    a = np.arange(P)
    k[:, K_ID:K_ID + P] = np.eye(P)
    k[:, K_LESS:K_LESS + P] = a[:, None] < a[None, :]
    k[:, K_HEAD:K_HEAD + P] = a[:, None] // HEAD == a[None, :] // HEAD
    e = np.arange(E0)
    k[:, K_FIRST:K_FIRST + E0] = E0 - e
    k[:, K_FULL:K_FULL + E0 * E0] = np.tile(P * e, E0)
    k[:, K_UPTO:K_UPTO + E0 * E0] = (e[None, :] <= e[:, None]).reshape(-1)
    k[:, K_BLOCK:K_BLOCK + E0 * BLOCKS] = np.repeat(np.arange(BLOCKS), E0)
    return k


def gated_layers(nc, x, ctx_in, gates, skip, kp0, kp1, d1, rw0, gu0, dn0, sgu0, sdn0, rw1, w1, ws1, cst,
                 out):
    st = ExitStack()
    with st:
        def sb(name, shape, dt=F32):
            return st.enter_context(nc.sbuf_tensor(name, shape, dt))

        def sem(name):
            return st.enter_context(nc.semaphore(name))

        ffn0 = ExitStack()

        def sb0(name, shape, dt=F32):
            return ffn0.enter_context(nc.sbuf_tensor(name, shape, dt))

        kp1d = nc.dram_tensor("kp1d", [H, KP], F32, kind="Internal").ap()
        xsort = nc.dram_tensor("xsort", [SLOTS, L], F32, kind="Internal").ap()
        ysort = nc.dram_tensor("ysort", [SLOTS, L], F32, kind="Internal").ap()
        wtok = nc.dram_tensor("wtok", [R1, TOK], F32, kind="Internal").ap()

        X = sb("X", [P, B, L])
        CN = sb("CN", [P, B, L])
        CR = sb("CR", [P, B, LT, P])
        XN = sb("XN", [P, B, L])
        XS = sb("XS", [P, B, L])
        CT = sb("CT", [P, LT * B, C])
        CRT = sb("CRT", [P, LT * B, C])
        VT = sb("VT", [P, LT * B, C])
        OT = sb("OT", [P, LT * B, C])
        TW = sb("TW", [P, 4, L])
        KV = sb("KV", [P, 2, LT * B * PAIRS])
        Z = sb("Z", [P, 2, LT * B * PAIRS])
        K = sb("K", [P, K_COLS])
        lessb = sb("lessb", [P, P], BF16)
        onesb = sb("onesb", [P, P], BF16)
        skipc = sb("skipc", [P, 1])
        hskip = sb("hskip", [P, P])
        gt = sb("gt", [P, 4])
        gin = sb("gin", [P, 4])
        kpt = sb("kpt", [H, KP])
        dt1 = sb("dt1", [H, 1])
        neghalf = sb("neghalf", [P, B])
        stt = sb("stt", [P, B, 6])
        mv = sb("mv", [P, B, 2])
        ve = sb("ve", [P, B])
        rstd = sb("rstd", [P, B])
        RW1 = sb("RW1", [P, LT, R1])
        WS = sb("WS", [P, LT * P + L])
        WR = sb("WR", [P, 2, WCOLS])
        RW0 = sb0("RW0", [P, LT, E0])
        GU0 = sb0("GU0", [P, E0, LT, 2 * F0])
        DN0 = sb0("DN0", [P, E0, F0 // P, L])
        SGU0 = sb0("SGU0", [P, LT, 2 * F0])
        SDN0 = sb0("SDN0", [P, F0 // P, L])
        HS = sb0("HS", [P, 2, 512])
        LG = sb0("LG", [P, B, E0])
        eqm = sb0("eqm", [P, B, E0])
        mx = sb0("mx", [P, B])
        pick = sb0("pick", [P, B])
        oh = sb0("oh", [P, B, E0], BF16)
        ex = sb0("ex", [P, B])
        score = sb0("score", [P, B])
        cmpk = sb0("cmpk", [P, E0, E0])
        nblk = sb0("nblk", [P, E0])
        upto = sb0("upto", [P, E0])
        start0 = sb0("start0", [P, E0])
        blke = sb0("blke", [1, BLOCKS, E0])
        blkf = sb0("blkf", [1, BLOCKS])
        blki = sb0("blki", [1, BLOCKS], I32)
        slotm = sb0("slotm", [P, B, E0])
        slotf = sb0("slotf", [P, B])
        sloti = sb0("sloti", [P, B], I32)
        zero = sb0("zero", [P, L])
        XB = sb0("XB", [P, 2, L])
        XBT = sb0("XBT", [P, 2, LT, P])
        SG = sb0("SG", [P, 2, F0])
        HB = sb0("HB", [P, 2, F0])
        HBT = sb0("HBT", [P, 2, F0 // P, P])
        YB = sb0("YB", [P, 2, L])

        ffn0.close()
        XH = sb("XH", [P, LT * B, C], F32R)
        XL = sb("XL", [P, LT * B, C], F32R)
        WSH = sb("WSH", [P, LT * P + L], F32R)
        WSL = sb("WSL", [P, LT * P + L], F32R)
        WH = sb("WH", [P, 2, WCOLS], F32R)
        WL = sb("WL", [P, 2, WCOLS], F32R)
        WB = sb("WB", [P, 2, TOK])
        WBS = sb("WBS", [I1, TOK])
        SI = sb("SI", [P, NT, 512])
        MU = sb("MU", [P, NT, 512])
        TK = sb("TK", [P, NT, 512])
        HI = sb("HI", [P, NT, 512], F32R)
        LO = sb("LO", [P, NT, 512], F32R)
        LG1 = sb("LG1", [P, B, R1])
        top = sb("top", [P, B, 8])
        rest = sb("rest", [P, B, E1])
        keep = sb("keep", [P, B, E1])
        ex1 = sb("ex1", [P, B, E1])
        exs = sb("exs", [P, B])
        den = sb("den", [P, B])
        rden = sb("rden", [P, B])
        W1 = sb("W1", [P, B, R1])
        WTS = sb("WTS", [R1, TOK])

        PS = st.enter_context(nc.psum_tensor("PS", [P, 8, 512], F32))
        ident = K[:, K_ID:K_ID + P]

        s_in = {n: sem("in_" + n) for n in ("x", "ctx", "cst", "small", "kp1", "kp1d", "rw", "sh0", "zero", "rw1", "ws1", "wtok", "wbs",
                                           "out")}
        s_w0 = [sem(f"in_w0_{e}") for e in range(2)]
        s_T = [[sem(f"in_toeplitz{a}_{u}") for u in range(4)] for a in range(2)]
        s_const = sem("constants_made")
        s_d1 = sem("d_added")
        s_dve = sem("vector_steps")
        s_gates = sem("gates_ready")
        s_var = [sem(f"variance{n}") for n in range(4)]
        s_rstd = [sem(f"rstd{n}") for n in range(4)]
        s_xn = [sem(f"normed{n}") for n in range(4)]
        s_rev = sem("ctx_reversed")
        s_tp0 = sem("turned_in_psum0")
        s_tp = [s_tp0] + [sem(f"turned_in_psum{n}") for n in (1, 2, 3)]
        s_tv = [sem(f"turned{n}") for n in range(4)]
        s_vc = sem("v_times_ctx")
        s_skip = sem("skip_sums")
        s_kv = [sem(f"kv{a}") for a in range(2)]
        s_conv = [sem(f"conv{a}") for a in range(2)]
        s_z = [sem(f"times_query{a}") for a in range(2)]
        s_red = [sem(f"summed{a}") for a in range(2)]
        s_back = [sem(f"back_in_psum{a}") for a in range(2)]
        s_res = [sem(f"residual{a}") for a in range(2)]
        s_lg = sem("logits0")
        s_mx = sem("best_logit")
        s_ex = sem("exp_best")
        s_oh = sem("onehot")
        s_pos = sem("positions")
        s_slot = sem("slots")
        s_xs = sem("scaled_tokens")
        s_scat = sem("scattered")
        s_shgu = sem("shared_gu")
        s_shsi = sem("shared_silu")
        s_shh = sem("shared_hidden")
        s_shdn = sem("shared_down")
        s_shadd = sem("shared_added")
        s_bx = sem("block_turned_psum")
        s_bxt = sem("block_turned")
        s_bgu = sem("block_gu")
        s_bsi = sem("block_silu")
        s_bh = sem("block_hidden")
        s_bhp = sem("block_hidden_psum")
        s_bht = sem("block_hidden_turned")
        s_bdn = sem("block_down")
        s_by = sem("block_y")
        s_byo = [sem(f"block_stored{i}") for i in range(2)]
        s_xb = [sem(f"in_block{i}") for i in range(2)]
        s_yg = [sem(f"gathered{b}") for b in range(B)]
        s_raw = [sem(f"in_raw{i}") for i in range(2)]
        s_wb = [sem(f"in_weights_of_tokens{i}") for i in range(2)]
        s_x1 = sem("x_split")
        s_lg1 = sem("logits1")
        s_e1 = sem("exp_in")
        s_ee = sem("exp_out")
        s_w1 = sem("token_weights")
        s_wt = sem("token_weights_psum")
        s_wts = sem("token_weights_turned")
        s_wsh = sem("shared1_high")
        s_wsl = sem("shared1_low")
        s_sgu = sem("shared1_gu")
        s_ssi = sem("shared1_silu")
        s_stw = sem("shared1_weighted")
        s_shi = sem("shared1_hi")
        s_slo = sem("shared1_lo")
        s_sdn = sem("shared1_down")
        s_wh = [sem("pair_high_up"), sem("pair_high_down")]
        s_wl = [sem("pair_low_up"), sem("pair_low_down")]
        s_gu = sem("pair_gu")
        s_si = sem("pair_silu")
        s_mul = sem("pair_product")
        s_tw = sem("pair_weighted")
        s_hi = sem("pair_hi")
        s_lo = sem("pair_lo")
        s_dn = sem("pair_down")
        s_acc = sem("sum_out_of_psum")
        s_fin = sem("final_psum")
        s_end = sem("final")
        block = st.enter_context(nc.Block())

        x_n = x.rearrange("b c l -> c b l")
        c_n = ctx_in.rearrange("b c l -> c b l")
        out_n = out.rearrange("b c l -> c b l")

        def bank(i, n=512):
            return PS[:, i, 0:n]

        def head(t, h):
            return t[:, :, bass.ds(HEAD * h, HEAD)]

        def over_j(ap):
            return ap.unsqueeze(3).broadcast_to([P, LT * B, HEAD, HEAD])

        def over_i(ap):
            return ap.unsqueeze(2).broadcast_to([P, LT * B, HEAD, HEAD])

        def pairs(ap):
            return ap.rearrange("p (a i j) -> p a i j", i=HEAD, j=HEAD)

        def head_runs(eng, body):
            body(0, True)
            with eng.Fori(1, H // GROUP) as i:
                body(i, False)

        @block.sync
        def _(sp):
            for half in range(2):
                sp.dma_start(X[:, 4 * half:4 * half + 4, :], x_n[:, 4 * half:4 * half + 4, :]).then_inc(s_in["x"], 16)
            sp.dma_start(CN[:, :, :], c_n).then_inc(s_in["ctx"], 16)

            def toeplitz(a, kp, h, u):
                rows = bass.AP(tensor=kp.tensor, offset=0, ap=[[KP, H], [1, P], [1, L]])
                sp.dma_start(TW[:, u:u + 1, :], rows[bass.ds(h, 1), :, :].rearrange("o p l -> p o l")
                             ).then_inc(s_T[a][u], 16)

            for a, kp in ((0, kp0), (1, kp1d)):
                if a:
                    sp.wait_ge(s_in["kp1d"], 16)
                for u in range(4):
                    if a:
                        sp.wait_ge(s_conv[0], H)
                    toeplitz(a, kp, u, u)
                with sp.Fori(1, H // GROUP) as i:
                    for u in range(4):
                        sp.wait_ge(s_conv[a], GROUP * i + (u - 3))
                        toeplitz(a, kp, GROUP * i + u, u)
                if a == 0:
                    sp.wait_ge(s_scat, 16 * B)
                    xs_r = xsort.rearrange("(j p) l -> p j l", p=P)

                    def load_x(j, par):
                        sp.dma_start(XB[:, par:par + 1, :], xs_r[:, bass.ds(j, 1), :]).then_inc(s_xb[par], 16)

                    def step(j, par):
                        sp.wait_ge(s_bx, j + 1)
                        load_x(j + 2, par)

                    load_x(0, 0)
                    load_x(1, 1)
                    with sp.Fori(0, BLOCKS // 2 - 1) as i:
                        for par in range(2):
                            step(2 * i + par, par)
                    step(BLOCKS - 3, 0)

            def raw(p, u):
                sp.dma_start(WR[:, u:u + 1, :], w1[bass.ds(p, 1), :, :].rearrange("o p n -> p o n")
                             ).then_inc(s_raw[u], 16)

            def token_weights(p, u):
                rows = bass.AP(tensor=wtok.tensor, offset=0, ap=[[TOK, R1], [0, I1], [1, TOK]])
                for e in range(2):
                    sp.dma_start(WB[I1 * e:I1 * e + I1, u:u + 1, :],
                                 rows[bass.ds(2 * p + e, 1), :, :].rearrange("o p t -> p o t")
                                 ).then_inc(s_wb[u], 16)

            raw(0, 0)
            raw(1, 1)
            sp.wait_ge(s_in["wtok"], 16)
            sp.dma_start(WBS[:, :], wtok[E1:E1 + 1, :].partition_broadcast(I1)).then_inc(s_in["wbs"], 16)
            token_weights(0, 0)
            token_weights(1, 1)
            with sp.Fori(1, NP1 // 2) as i:
                for u in range(2):
                    p = 2 * i + u
                    sp.wait_ge(s_wl[0], p - 1)
                    sp.wait_ge(s_wl[1], p - 1)
                    raw(p, u)
                    sp.wait_ge(s_tw, 2 * p - 2)
                    token_weights(p, u)
            for q in range(4):
                sp.wait_ge(s_end, q + 1)
                sp.dma_start(out_n[:, 2 * q:2 * q + 2, :], X[:, 2 * q:2 * q + 2, :]).then_inc(s_in["out"], 16)
            sp.wait_ge(s_in["out"], 64)

        @block.gpsimd
        def _(pool):
            pool.memset(neghalf[:], -0.5).then_inc(s_const, 1)
            pool.memset(onesb[:], 1.0).then_inc(s_const, 1)
            pool.memset(zero[:], 0.0).then_inc(s_const, 1)

            def rstd_of(n):
                pool.wait_ge(s_const, 1)
                pool.wait_ge(s_var[n], 1)
                if n:
                    pool.wait_ge(s_rstd[n - 1], 1)
                pool.tensor_tensor(rstd[:], ve[:], neghalf[:], ALU.pow).then_inc(s_rstd[n], 1)

            def products(a, left, right):
                def body(i, first):
                    for u in range(GROUP):
                        h = GROUP * i + u
                        if not first or u >= 2:
                            pool.wait_ge(s_conv[a], h - 1)
                        pool.tensor_tensor(pairs(KV[:, u % 2, :]), over_j(head(left, h)), over_i(head(right, h)),
                                           ALU.mult).then_inc(s_kv[a], 1)
                head_runs(pool, body)

            rstd_of(0)
            pool.wait_ge(s_tv[0], 12)
            products(0, VT, CRT)
            rstd_of(1)
            pool.wait_ge(s_slot, 2)
            pool.wait_ge(s_in["zero"], 16)
            for b in range(B):
                pool.wait_ge(s_xs, b + 1)
                pool.indirect_dma_start(out=xsort, out_offset=bass.IndirectOffsetOnAxis(ap=sloti[:, b:b + 1], axis=0),
                                        in_=XS[:, b, :], in_offset=None).then_inc(s_scat, 16)
            ys_r = ysort.rearrange("(j p) l -> p j l", p=P)

            def store_y(j, par):
                pool.wait_ge(s_by, j + 1)
                pool.dma_start(ys_r[:, bass.ds(j, 1), :], YB[:, par:par + 1, :]).then_inc(s_byo[par], 16)

            with pool.Fori(0, BLOCKS // 2) as i:
                for par in range(2):
                    store_y(2 * i + par, par)
            store_y(BLOCKS - 1, 0)
            pool.wait_ge(s_byo[0], 16 * ((BLOCKS + 1) // 2))
            pool.wait_ge(s_byo[1], 16 * (BLOCKS // 2))
            pool.wait_ge(s_scat, 16 * B)
            for b in range(B):
                pool.indirect_dma_start(out=XS[:, b, :], out_offset=None, in_=ysort,
                                        in_offset=bass.IndirectOffsetOnAxis(ap=sloti[:, b:b + 1], axis=0)
                                        ).then_inc(s_yg[b], 16)
            rstd_of(2)
            pool.wait_ge(s_conv[0], H)
            products(1, CRT, CRT)
            rstd_of(3)
            pool.wait_ge(s_wsh, 1)
            pool.tensor_tensor(WSL[:, :], WS[:, :], WSH[:, :].bitcast(F32), ALU.subtract).then_inc(s_wsl, 1)
            with pool.Fori(0, NP1 // 2) as i:
                for u in range(2):
                    for part in range(2):
                        pool.wait_ge(s_wh[part], 2 * i + u + 1)
                        w = WPARTS[part]
                        pool.tensor_tensor(WL[:, u, w], WR[:, u, w], WH[:, u, w].bitcast(F32), ALU.subtract
                                           ).then_inc(s_wl[part], 1)

        @block.scalar
        def _(act):
            act.dma_start(K[:, :], cst).then_inc(s_in["cst"], 16)
            act.dma_start(gin[:, :], gates.partition_broadcast(P)).then_inc(s_in["small"], 16)
            act.dma_start(skipc[:, :], skip).then_inc(s_in["small"], 16)
            act.dma_start(kpt[:, :], kp1).then_inc(s_in["kp1"], 16)
            act.dma_start(dt1[:, :], d1).then_inc(s_in["kp1"], 16)
            act.dma_start(RW0[:, :, :], rw0.rearrange("(k p) e -> p k e", p=P)).then_inc(s_in["rw"], 16)
            act.dma_start(SGU0[:, :, :], sgu0.rearrange("(k p) f -> p k f", p=P)).then_inc(s_in["sh0"], 16)
            act.dma_start(SDN0[:, :, :], sdn0.rearrange("(k p) f -> p k f", p=P)).then_inc(s_in["sh0"], 16)
            for e in range(E0):
                act.dma_start(GU0[:, e, :, :], gu0[e].rearrange("(k p) f -> p k f", p=P)).then_inc(s_w0[0], 16)
                act.dma_start(DN0[:, e, :, :], dn0[e].rearrange("(k p) f -> p k f", p=P)).then_inc(s_w0[1], 16)
            act.dma_start(RW1[:, :, :], rw1.rearrange("(k p) e -> p k e", p=P)).then_inc(s_in["rw1"], 16)
            act.dma_start(WS[:, :], ws1).then_inc(s_in["ws1"], 16)
            act.wait_ge(s_const, 3)
            act.dma_start(xsort.rearrange("(j p) l -> p j l", p=P),
                          zero[:].unsqueeze(1).broadcast_to([P, BLOCKS, L])).then_inc(s_in["zero"], 16)
            act.wait_ge(s_d1, 1)
            act.dma_start(kp1d, kpt[:, :]).then_inc(s_in["kp1d"], 16)
            act.wait_ge(s_in["ctx"], 16)
            for half in range(2):
                b = slice(4 * half, 4 * half + 4)
                act.activation(CR[:, b, :, :], CN[:, b, :].rearrange("c b (t m) -> c b t m", t=LT)[:, :, :, ::-1],
                               ACT.Copy).then_inc(s_rev, 1)
            act.wait_ge(s_in["cst"], 16)
            act.activation(lessb[:, :], K[:, K_LESS:K_LESS + P], ACT.Copy).then_inc(s_rev, 1)
            act.wait_ge(s_in["small"], 32)
            act.activation(gt[:, :], gin[:, :], ACT.Tanh).then_inc(s_gates, 1)

            def out_of_psum(n, dst, first, groups, base):
                for q in range(groups):
                    act.wait_ge(s_tp[n], first + q + 1)
                    t, half = q % 2, q // 2
                    act.activation(dst[:, t * B + 4 * half:t * B + 4 * half + 4, :],
                                   PS[:, base + q, :].rearrange("p (b c) -> p b c", b=4), ACT.Copy
                                   ).then_inc(s_tv[n], 1)

            out_of_psum(0, CRT, 0, 4, 0)
            out_of_psum(0, CT, 4, 4, 4)
            out_of_psum(0, VT, 8, 4, 0)
            out_of_psum(1, VT, 0, 4, 0)
            act.wait_ge(s_mx, 1)
            act.activation(ex[:, :], mx[:, :], ACT.Exp, scale=-1.0).then_inc(s_ex, 1)
            for n in range(2):
                act.wait_ge(s_shgu, n + 1)
                if n:
                    act.wait_ge(s_shdn, n)
                for f in range(2):
                    act.activation(HS[:, f, :], bank(f), ACT.Silu).then_inc(s_shsi, 1)

            def turn_block(j, par, first):
                act.wait_ge(s_bx, j + 1)
                if not first:
                    act.wait_ge(s_bgu, j - 1)
                act.activation(XBT[:, par, :, :], PS[:, par, 0:L].rearrange("p (k s) -> p k s", k=LT), ACT.Copy
                               ).then_inc(s_bxt, 1)

            def silu_block(j, par, first):
                act.wait_ge(s_bgu, j + 1)
                if not first:
                    act.wait_ge(s_bh, j - 1)
                act.activation(SG[:, par, :], PS[:, 4 + par, 0:F0], ACT.Silu).then_inc(s_bsi, 1)

            turn_block(0, 0, True)
            silu_block(0, 0, True)
            turn_block(1, 1, True)

            def step(i, u, first):
                j = 2 * i + u
                silu_block(j + 1, 1 - u, first and u == 0)
                turn_block(j + 2, u, False)
                act.wait_ge(s_bdn, j + 1)
                if not first:
                    act.wait_ge(s_byo[u], 16 * i)
                act.activation(YB[:, u, :], PS[:, 6 + u, 0:L], ACT.Copy).then_inc(s_by, 1)

            for u in range(2):
                step(0, u, True)
            with act.Fori(1, BLOCKS // 2 - 1) as i:
                for u in range(2):
                    step(i, u, False)
            for j in range(BLOCKS - 3, BLOCKS):
                if j + 1 < BLOCKS:
                    silu_block(j + 1, (j + 1) % 2, False)
                if j + 2 < BLOCKS:
                    turn_block(j + 2, j % 2, False)
                act.wait_ge(s_bdn, j + 1)
                act.wait_ge(s_byo[j % 2], 16 * (j // 2))
                act.activation(YB[:, j % 2, :], PS[:, 6 + j % 2, 0:L], ACT.Copy).then_inc(s_by, 1)

            out_of_psum(2, VT, 0, 4, 0)

            out_of_psum(3, VT, 0, 4, 0)

            def high(part, p, u, first):
                act.wait_ge(s_raw[u], 16 * (p // 2 + 1) if isinstance(p, int) else first)
                if not isinstance(p, int) or p >= 2:
                    act.wait_ge((s_gu, s_dn)[part], 2 * p - 2)
                w = WPARTS[part]
                act.activation(WH[:, u, w], WR[:, u, w], ACT.Copy).then_inc(s_wh[part], 1)

            act.wait_ge(s_in["ws1"], 16)
            act.activation(WSH[:, :], WS[:, :], ACT.Copy).then_inc(s_wsh, 1)
            for part in range(2):
                high(part, 0, 0, None)
            act.wait_ge(s_e1, 1)
            act.activation(ex1[:, :, :], ex1[:, :, :], ACT.Exp).then_inc(s_ee, 1)
            act.activation(exs[:, :], LG1[:, :, E1], ACT.Exp, scale=-1.0).then_inc(s_ee, 1)
            for n in range(NT):
                act.wait_ge(s_sgu, n + 1)
                act.activation(SI[0:I1, n, :], PS[0:I1, 2 * n, :], ACT.Silu).then_inc(s_ssi, 1)
                act.activation(MU[0:I1, n, :], PS[I1:P, 2 * n, :], ACT.Copy).then_inc(s_ssi, 1)
            for n in range(2):
                act.wait_ge(s_wt, n + 1)
                act.activation(WTS[:, 512 * n:512 * n + 512], PS[0:R1, 4 + n, :], ACT.Copy).then_inc(s_wts, 1)
            act.wait_ge(s_wts, 2)
            act.dma_start(wtok, WTS[:, :]).then_inc(s_in["wtok"], 16)
            for n in range(NT):
                act.wait_ge(s_stw, n + 1)
                act.activation(HI[0:I1, n, :], TK[0:I1, n, :], ACT.Copy).then_inc(s_shi, 1)

            def pair(p, u, first, more, nxt):
                for n in range(NT):
                    act.wait_ge(s_gu, 2 * p + n + 1)
                    if not first:
                        act.wait_ge(s_mul, 2 * p + n - 1)
                    act.activation(SI[:, n, :], bank(2 * n), ACT.Silu).then_inc(s_si, 1)
                    if n == 0 and more:
                        high(0, p + 1, 1 - u, nxt)
                    act.wait_ge(s_tw, 2 * p + n + 1)
                    if first:
                        act.wait_ge(s_sdn, n + 1)
                    else:
                        act.wait_ge(s_dn, 2 * p + n - 1)
                    act.activation(HI[:, n, :], TK[:, n, :], ACT.Copy).then_inc(s_hi, 1)
                    if n == 1 and more:
                        high(1, p + 1, 1 - u, nxt)

            pair(0, 0, True, True, None)
            pair(1, 1, False, True, None)
            with act.Fori(1, NP1 // 2 - 1) as i:
                pair(2 * i, 0, False, True, 16 * (i + 1))
                pair(2 * i + 1, 1, False, True, 16 * (i + 2))
            pair(NP1 - 2, 0, False, True, None)
            pair(NP1 - 1, 1, False, False, None)
            act.wait_ge(s_dn, 2 * NP1)
            for n in range(NT):
                act.activation(OT[:, 4 * n:4 * n + 4, :].rearrange("p b c -> p (b c)"), bank(4 + n), ACT.Copy
                               ).then_inc(s_acc, 1)

        @block.vector
        def _(dve):
            n_own = [0]

            def own(ins):
                n_own[0] += 1
                ins.then_inc(s_dve, 1)

            def settle():
                dve.wait_ge(s_dve, n_own[0])

            def norm_stats(n, ready=None):
                for b in range(B):
                    if ready:
                        ready(b)
                    own(dve.bn_stats(stt[:, b, :], X[:, b, :]))
                settle()
                for b in range(B):
                    own(dve.bn_aggr(mv[:, b, :], stt[:, b, :]))
                settle()
                dve.tensor_scalar_add(ve[:], mv[:, :, 1], EPS).then_inc(s_var[n], 1)
                dve.wait_ge(s_rstd[n], 1)

            def normed(n, b, dst):
                dve.tensor_scalar(dst, X[:, b, :].rearrange("c (t m) -> c t m", t=LT), mv[:, b, 0:1],
                                  rstd[:, b:b + 1], ALU.subtract, ALU.mult).then_inc(s_xn[n], 1)

            dve.wait_ge(s_in["kp1"], 32)
            dve.tensor_tensor(kpt[:, PAD:PAD + 1], kpt[:, PAD:PAD + 1], dt1[:, :], ALU.add).then_inc(s_d1, 1)

            norm_stats(0, lambda b: dve.wait_ge(s_in["x"], 32) if b == 0 else None)
            for b in range(B):
                normed(0, b, XN[:, b, :].rearrange("c (t m) -> c t m", t=LT)[:, :, ::-1])
            dve.wait_ge(s_in["cst"], 16)
            dve.wait_ge(s_in["small"], 32)
            dve.wait_ge(s_rev, 3)
            dve.wait_ge(s_xn[0], B)
            own(dve.tensor_scalar(hskip[:, :], K[:, K_HEAD:K_HEAD + P], skipc[:, 0:1], None, ALU.mult))
            CRf = CR[:, :, :, :].rearrange("c b t m -> c b (t m)")
            dve.tensor_tensor(XS[:, :, :], XN[:, :, :], CRf, ALU.mult).then_inc(s_vc, 1)
            dve.wait_ge(s_gates, 1)
            for q in range(4):
                b = slice(2 * q, 2 * q + 2)
                dve.wait_ge(s_skip, q + 1)
                own(dve.tensor_tensor(XS[:, b, :], bank(4 + q).rearrange("c (b l) -> c b l", b=2), CRf[:, b, :],
                                      ALU.mult))
            settle()
            for b in range(B):
                own(dve.scalar_tensor_tensor(
                    X[:, b, :].rearrange("c (t m) -> c t m", t=LT),
                    XS[:, b, :].rearrange("c (t m) -> c t m", t=LT)[:, :, ::-1], gt[:, 0:1],
                    X[:, b, :].rearrange("c (t m) -> c t m", t=LT), ALU.mult, ALU.add))

            def combine(a, query):
                def body(i, first):
                    for u in range(GROUP):
                        h = GROUP * i + u
                        dve.wait_ge(s_conv[a], h + 1)
                        if not first or u >= 2:
                            dve.wait_ge(s_red[a], h - 1)
                        y = PS[:, 2 * (u % 2):2 * (u % 2) + 2, :].rearrange("p t n -> p (t n)")
                        z = Z[:, u % 2, :]
                        dve.tensor_tensor(pairs(z), pairs(y), over_j(head(query, h)), ALU.mult).then_inc(s_z[a], 1)
                        dve.wait_ge(s_z[a], h + 1)
                        dve.tensor_reduce(head(OT, h), pairs(z).rearrange("p a i j -> p a j i"), AX.X, ALU.add
                                          ).then_inc(s_red[a], 1)
                head_runs(dve, body)

            def add_back(a, g):
                for q in range(4):
                    dve.wait_ge(s_back[a], q + 1)
                    own(dve.scalar_tensor_tensor(X[:, 2 * q:2 * q + 2, :].rearrange("c b l -> c (b l)"), bank(4 + q),
                                                 g, X[:, 2 * q:2 * q + 2, :].rearrange("c b l -> c (b l)"),
                                                 ALU.mult, ALU.add))
                settle()

            dve.wait_ge(s_tv[0], 12)
            settle()
            combine(0, CT)
            add_back(0, gt[:, 0:1])

            norm_stats(1)
            for b in range(B):
                normed(1, b, XN[:, b, :].rearrange("c (t m) -> c t m", t=LT))
            dve.wait_ge(s_lg, 1)
            own(dve.tensor_copy(LG[:, :, :], PS[:, 4, 0:B * E0].rearrange("p (b e) -> p b e", b=B)))
            settle()
            dve.tensor_reduce(mx[:, :], LG[:, :, :], AX.X, ALU.max).then_inc(s_mx, 1)
            dve.wait_ge(s_mx, 1)
            own(dve.tensor_tensor(eqm[:, :, :], LG[:, :, :], mx[:].unsqueeze(2).broadcast_to([P, B, E0]),
                                  ALU.is_equal))
            settle()
            own(dve.tensor_tensor(LG[:, :, :], eqm[:, :, :],
                                  K[:, K_FIRST:K_FIRST + E0].unsqueeze(1).broadcast_to([P, B, E0]), ALU.mult))
            settle()
            own(dve.tensor_reduce(pick[:, :], LG[:, :, :], AX.X, ALU.max))
            settle()
            dve.tensor_tensor(oh[:, :, :], LG[:, :, :], pick[:].unsqueeze(2).broadcast_to([P, B, E0]),
                              ALU.is_equal).then_inc(s_oh, 1)
            dve.wait_ge(s_ex, 1)
            own(dve.tensor_scalar_add(ex[:, :], ex[:, :], 1.0))
            settle()
            own(dve.reciprocal(score[:, :], ex[:, :]))
            settle()
            dve.wait_ge(s_xn[1], B)
            for b in range(B):
                dve.tensor_scalar(XS[:, b, :], XN[:, b, :], score[:, b:b + 1], None, ALU.mult).then_inc(s_xs, 1)
            dve.wait_ge(s_pos, 1)
            cnt = PS[:, 5, B * E0:B * E0 + E0]
            own(dve.tensor_tensor(cmpk[:, :, :], cnt.unsqueeze(2).broadcast_to([P, E0, E0]),
                                  K[:, K_FULL:K_FULL + E0 * E0].rearrange("p (e k) -> p e k", e=E0), ALU.is_gt))
            settle()
            own(dve.tensor_reduce(nblk[:, :], cmpk[:, :, :], AX.X, ALU.add))
            settle()
            own(dve.tensor_tensor(cmpk[:, :, :], nblk[:].unsqueeze(1).broadcast_to([P, E0, E0]),
                                  K[:, K_UPTO:K_UPTO + E0 * E0].rearrange("p (e k) -> p e k", e=E0), ALU.mult))
            settle()
            own(dve.tensor_reduce(upto[:, :], cmpk[:, :, :], AX.X, ALU.add))
            settle()
            own(dve.tensor_tensor(start0[:, :], upto[:, :], nblk[:, :], ALU.subtract))
            settle()
            own(dve.tensor_scalar(start0[:, :], start0[:, :], float(P), None, ALU.mult))
            settle()
            own(dve.tensor_tensor(slotm[:, :, :], PS[:, 5, 0:B * E0].rearrange("p (b e) -> p b e", b=B),
                                  start0[:].unsqueeze(1).broadcast_to([P, B, E0]), ALU.add))
            settle()
            own(dve.tensor_tensor(slotm[:, :, :], slotm[:, :, :], oh[:, :, :], ALU.mult))
            settle()
            own(dve.tensor_reduce(slotf[:, :], slotm[:, :, :], AX.X, ALU.add))
            settle()
            dve.tensor_copy(sloti[:, :], slotf[:, :]).then_inc(s_slot, 1)
            own(dve.tensor_tensor(blke[:, :, :], upto[0:1, :].unsqueeze(1).broadcast_to([1, BLOCKS, E0]),
                                  K[0:1, K_BLOCK:K_BLOCK + E0 * BLOCKS].rearrange("p (j e) -> p j e", e=E0),
                                  ALU.is_le))
            settle()
            own(dve.tensor_reduce(blkf[:, :], blke[:, :, :], AX.X, ALU.add))
            settle()
            own(dve.tensor_scalar_min(blkf[:, :], blkf[:, :], float(E0 - 1)))
            settle()
            dve.tensor_copy(blki[:, :], blkf[:, :]).then_inc(s_slot, 1)
            for n in range(2):
                for f in range(2):
                    dve.wait_ge(s_shsi, 2 * n + f + 1)
                    dve.tensor_tensor(HS[:, f, :], HS[:, f, :], bank(2 + f), ALU.mult).then_inc(s_shh, 1)
                for q in range(2):
                    dve.wait_ge(s_shdn, n + 1)
                    b = slice(4 * n + 2 * q, 4 * n + 2 * q + 2)
                    dve.scalar_tensor_tensor(X[:, b, :].rearrange("c b l -> c (b l)"), bank(6 + q), gt[:, 1:2],
                                             X[:, b, :].rearrange("c b l -> c (b l)"), ALU.mult, ALU.add
                                             ).then_inc(s_shadd, 1)

            def hidden(i, u, first, j=None):
                j = 2 * i + u if j is None else j
                dve.wait_ge(s_bsi, j + 1)
                if not first:
                    dve.wait_ge(s_bhp, j - 1)
                dve.tensor_tensor(HB[:, u, :], SG[:, u, :], PS[:, 4 + u, F0:2 * F0], ALU.mult).then_inc(s_bh, 1)
                dve.wait_ge(s_bhp, j + 1)
                if not first:
                    dve.wait_ge(s_bdn, j - 1)
                dve.tensor_copy(HBT[:, u, :, :], PS[:, 2 + u, 0:F0].rearrange("p (k s) -> p k s", k=F0 // P)
                                ).then_inc(s_bht, 1)

            for u in range(2):
                hidden(0, u, True)
            with dve.Fori(1, BLOCKS // 2) as i:
                for u in range(2):
                    hidden(i, u, False)
            hidden(0, (BLOCKS - 1) % 2, False, BLOCKS - 1)

            def gathered(b):
                dve.wait_ge(s_yg[b], 16)
                if b == 0:
                    dve.wait_ge(s_shadd, 4)
                own(dve.scalar_tensor_tensor(X[:, b, :], XS[:, b, :], gt[:, 1:2], X[:, b, :], ALU.mult, ALU.add))
                settle()

            norm_stats(2, gathered)
            for b in range(B):
                normed(2, b, XN[:, b, :].rearrange("c (t m) -> c t m", t=LT))
            dve.wait_ge(s_tv[2], 4)
            dve.wait_ge(s_red[0], H)
            combine(1, VT)
            add_back(1, gt[:, 2:3])

            norm_stats(3)
            for b in range(B):
                normed(3, b, XN[:, b, :].rearrange("c (t m) -> c t m", t=LT))
            for q in range(4):
                dve.wait_ge(s_tv[3], q + 1)
                part = slice((q % 2) * B + 4 * (q // 2), (q % 2) * B + 4 * (q // 2) + 4)
                own(dve.tensor_copy(XH[:, part, :], VT[:, part, :]))
                settle()
                dve.tensor_tensor(XL[:, part, :], VT[:, part, :], XH[:, part, :].bitcast(F32), ALU.subtract
                                  ).then_inc(s_x1, 1)
            for n in range(2):
                dve.wait_ge(s_lg1, n + 1)
                own(dve.tensor_copy(LG1[:, 4 * n:4 * n + 4, :],
                                    PS[:, 4 + n, 0:4 * R1].rearrange("p (b e) -> p b e", b=4)))
            settle()
            for b in range(B):
                own(dve.max(top[:, b, :], LG1[:, b, 0:E1]))
            settle()
            dve.tensor_tensor(ex1[:, :, :], LG1[:, :, 0:E1], top[:, :, 0:1].broadcast_to([P, B, E1]), ALU.subtract
                              ).then_inc(s_e1, 1)
            for b in range(B):
                own(dve.match_replace(rest[:, b, :], top[:, b, :], LG1[:, b, 0:E1], -3.0e38))
            settle()
            own(dve.tensor_tensor(keep[:, :, :], rest[:, :, :], LG1[:, :, 0:E1], ALU.not_equal))
            settle()
            dve.wait_ge(s_ee, 2)
            own(dve.tensor_tensor(keep[:, :, :], keep[:, :, :], ex1[:, :, :], ALU.mult))
            own(dve.tensor_scalar_add(exs[:, :], exs[:, :], 1.0))
            settle()
            own(dve.tensor_reduce(den[:, :], keep[:, :, :], AX.X, ALU.add))
            settle()
            own(dve.reciprocal(rden[:, :], den[:, :]))
            settle()
            dve.tensor_tensor(W1[:, :, 0:E1], keep[:, :, :], rden[:].unsqueeze(2).broadcast_to([P, B, E1]), ALU.mult
                              ).then_inc(s_w1, 1)
            dve.reciprocal(W1[:, :, E1], exs[:, :]).then_inc(s_w1, 1)
            own(dve.memset(HI[I1:P, :, :].bitcast(F32), 0.0))
            own(dve.memset(LO[I1:P, :, :].bitcast(F32), 0.0))
            settle()
            for n in range(NT):
                t = slice(512 * n, 512 * n + 512)
                dve.wait_ge(s_ssi, 2 * n + 2)
                own(dve.tensor_tensor(MU[0:I1, n, :], SI[0:I1, n, :], MU[0:I1, n, :], ALU.mult))
                settle()
                dve.wait_ge(s_in["wbs"], 16)
                dve.tensor_tensor(TK[0:I1, n, :], MU[0:I1, n, :], WBS[:, t], ALU.mult).then_inc(s_stw, 1)
            for n in range(NT):
                dve.wait_ge(s_shi, n + 1)
                dve.tensor_tensor(LO[0:I1, n, :], TK[0:I1, n, :], HI[0:I1, n, :].bitcast(F32), ALU.subtract
                                  ).then_inc(s_slo, 1)
            dve.wait_ge(s_slo, 2)

            def pair(i, u, first):
                p = 2 * i + u
                for n in range(NT):
                    dve.wait_ge(s_si, 2 * p + n + 1)
                    if not first or u:
                        dve.wait_ge(s_tw, 2 * p + n - 1 if not first or u or n else 1)
                    dve.tensor_tensor(MU[:, n, :], SI[:, n, :], bank(2 * n + 1), ALU.mult).then_inc(s_mul, 1)
                    dve.wait_ge(s_wb[u], 32 * (i + 1))
                    dve.wait_ge(s_mul, 2 * p + n + 1)
                    dve.tensor_tensor(TK[:, n, :], MU[:, n, :], WB[:, u, 512 * n:512 * n + 512], ALU.mult
                                      ).then_inc(s_tw, 1)
                    dve.wait_ge(s_hi, 2 * p + n + 1)
                    dve.tensor_tensor(LO[:, n, :], TK[:, n, :], HI[:, n, :].bitcast(F32), ALU.subtract
                                      ).then_inc(s_lo, 1)

            for u in range(2):
                pair(0, u, True)
            with dve.Fori(1, NP1 // 2) as i:
                for u in range(2):
                    pair(i, u, False)
            dve.wait_ge(s_dn, 2 * NP1)
            for n in range(NT):
                dve.tensor_copy(OT[:, B + 4 * n:B + 4 * n + 4, :].rearrange("p b c -> p (b c)"), bank(6 + n)
                                ).then_inc(s_acc, 1)
            for q in range(4):
                dve.wait_ge(s_fin, q + 1)
                xq = X[:, 2 * q:2 * q + 2, :].rearrange("c b l -> c (b l)")
                dve.scalar_tensor_tensor(xq, bank(q), gt[:, 3:4], xq, ALU.mult, ALU.add).then_inc(s_end, 1)

        @block.tensor
        def _(pe):
            def turn(n, src, ready, base, free=None):
                for q in range(4):
                    t, half = q % 2, q // 2
                    ready(half)
                    if free:
                        free(q)
                    for k in range(4):
                        last = pe.transpose(PS[:, base + q, P * k:P * k + P], src(4 * half + k, t), ident)
                    last.then_inc(s_tp[n], 1)

            pe.wait_ge(s_in["cst"], 16)
            turn(0, lambda b, t: CR[:, b, t, :], lambda half: pe.wait_ge(s_rev, half + 1), 0)
            turn(0, lambda b, t: CN[:, b, P * t:P * t + P], lambda half: None, 4)
            turn(0, lambda b, t: XN[:, b, P * t:P * t + P], lambda half: pe.wait_ge(s_xn[0], 4 * half + 4), 0,
                 lambda q: pe.wait_ge(s_tv[0], q + 1))
            pe.wait_ge(s_vc, 1)
            pe.wait_ge(s_tv[0], 8)
            for q in range(4):
                pe.matmul(bank(4 + q), hskip[:, :], XS[:, 2 * q:2 * q + 2, :].rearrange("c b l -> c (b l)"),
                          start=True, stop=True).then_inc(s_skip, 1)

            def convolve(a):
                def body(i, first):
                    for u in range(GROUP):
                        h = GROUP * i + u
                        pe.wait_ge(s_T[a][u], 16 * (i + 1))
                        pe.wait_ge(s_kv[a], h + 1)
                        if not first or u >= 2:
                            pe.wait_ge(s_z[a], h - 1)
                        y = 2 * (u % 2)
                        near, far = TW[:, u, 0:P], TW[:, u, P:2 * P]
                        early, late = KV[:, u % 2, 0:B * PAIRS], KV[:, u % 2, B * PAIRS:2 * B * PAIRS]
                        pe.matmul(bank(y), near, early, start=True, stop=True)
                        pe.matmul(bank(y + 1), near, late, start=True, stop=False)
                        pe.matmul(bank(y + 1), far, early, start=False, stop=True).then_inc(s_conv[a], 1)
                head_runs(pe, body)

            def back(a):
                pe.wait_ge(s_red[a], H)
                for q in range(4):
                    for k in range(4):
                        b, t = 2 * q + k // 2, k % 2
                        last = pe.transpose(PS[:, 4 + q, P * k:P * k + P], OT[:, t * B + b, :], ident)
                    last.then_inc(s_back[a], 1)

            pe.wait_ge(s_tv[0], 12)
            convolve(0)
            back(0)

            turn(1, lambda b, t: XN[:, b, P * t:P * t + P], lambda half: pe.wait_ge(s_xn[1], 4 * half + 4), 0)
            pe.wait_ge(s_tv[1], 4)
            pe.wait_ge(s_in["rw"], 16)
            for b in range(B):
                for k in range(LT):
                    last = pe.matmul(PS[:, 4, E0 * b:E0 * b + E0], VT[:, k * B + b, :], RW0[:, k, :], start=k == 0,
                                     stop=k == LT - 1)
            last.then_inc(s_lg, 1)

            def tokens(k, n):
                return VT[:, k * B + 4 * n:k * B + 4 * n + 4, :].rearrange("p b c -> p (b c)")

            def shared_up(n, f):
                for k in range(LT):
                    last = pe.matmul(bank(f), SGU0[:, k, P * f:P * f + P], tokens(k, n), start=k == 0,
                                     stop=k == LT - 1)
                return last

            def shared_down(n):
                pe.wait_ge(s_shh, 2 * n + 2)
                if n:
                    pe.wait_ge(s_shadd, 2)
                for b in range(4):
                    for k in range(2):
                        last = pe.matmul(PS[:, 6 + b // 2, L * (b % 2):L * (b % 2) + L], HS[:, k, P * b:P * b + P],
                                         SDN0[:, k, :], start=k == 0, stop=k == 1)
                last.then_inc(s_shdn, 1)

            pe.wait_ge(s_in["sh0"], 32)
            shared_up(0, 0)
            shared_up(0, 1)
            pe.wait_ge(s_oh, 1)
            pos = PS[:, 5, 0:B * E0]
            pe.matmul(pos, lessb[:, :], oh[:, :, :].rearrange("p b e -> p (b e)"), start=True, stop=True)
            for d in range(1, B):
                pe.matmul(PS[:, 5, E0 * d:B * E0], onesb[:, :], oh[:, 0:B - d, :].rearrange("p b e -> p (b e)"),
                          start=False, stop=True, skip_group_check=True)
            for b in range(B):
                last = pe.matmul(PS[:, 5, B * E0:B * E0 + E0], onesb[:, :], oh[:, b, :], start=False,
                                 stop=True, skip_group_check=True)
            last.then_inc(s_pos, 1)
            shared_up(0, 2)
            shared_up(0, 3).then_inc(s_shgu, 1)
            pe.wait_ge(s_shh, 2)
            for f in range(3):
                shared_up(1, f)
            shared_up(1, 3).then_inc(s_shgu, 1)
            shared_down(0)
            shared_down(1)

            def turn_block(j, par, first, loads):
                pe.wait_ge(s_xb[par], 16 * loads)
                if not first:
                    pe.wait_ge(s_bxt, j - 1)
                for k in range(LT):
                    last = pe.transpose(PS[:, par, P * k:P * k + P], XB[:, par, P * k:P * k + P], ident)
                last.then_inc(s_bx, 1)

            held = [pe.alloc_register(name=f"expert{par}") for par in range(2)]

            def read_expert(j, par):
                pe.reg_load(held[par], blki[0:1, j:j + 1] if isinstance(j, int) else blki[0:1, bass.ds(j, 1)])

            def expert(par):
                return pe.snap(held[par], min_val=0, max_val=E0 - 1)

            def up_block(j, par, e, first):
                pe.wait_ge(s_bxt, j + 1)
                if not first:
                    pe.wait_ge(s_bh, j - 1)
                for k in range(LT):
                    last = pe.matmul(bank(4 + par), XBT[:, par, k, :],
                                     GU0[:, bass.ds(e, 1), k, :].rearrange("p o f -> p (o f)"), start=k == 0,
                                     stop=k == LT - 1)
                last.then_inc(s_bgu, 1)

            def turn_hidden(j, par, first):
                pe.wait_ge(s_bh, j + 1)
                if not first:
                    pe.wait_ge(s_bht, j - 1)
                for k in range(F0 // P):
                    last = pe.transpose(PS[:, 2 + par, P * k:P * k + P], HB[:, par, P * k:P * k + P], ident)
                last.then_inc(s_bhp, 1)

            def down_block(j, par, e, first):
                pe.wait_ge(s_bht, j + 1)
                if not first:
                    pe.wait_ge(s_by, j - 1)
                for k in range(F0 // P):
                    last = pe.matmul(PS[:, 6 + par, 0:L], HBT[:, par, k, :],
                                     DN0[:, bass.ds(e, 1), k, :].rearrange("p o f -> p (o f)"), start=k == 0,
                                     stop=k == F0 // P - 1)
                last.then_inc(s_bdn, 1)

            pe.wait_ge(s_slot, 2)
            pe.wait_ge(s_w0[0], 16 * E0)
            pe.wait_ge(s_w0[1], 16 * E0)
            pe.wait_ge(s_shh, 4)
            pe.wait_ge(s_shadd, 4)

            def step(j, u, first, loads):
                turn_hidden(j, u, first)
                if not isinstance(j, int) or j + 1 < BLOCKS:
                    up_block(j + 1, 1 - u, expert(1 - u), first and u == 0)
                if not isinstance(j, int) or j + 2 < BLOCKS:
                    turn_block(j + 2, u, False, loads)
                down_block(j, u, expert(u), first)
                if not isinstance(j, int) or j + 2 < BLOCKS:
                    read_expert(j + 2, u)

            turn_block(0, 0, True, 1)
            read_expert(0, 0)
            up_block(0, 0, expert(0), True)
            read_expert(1, 1)
            turn_block(1, 1, True, 1)
            for u in range(2):
                step(u, u, True, 2)
            with pe.Fori(1, BLOCKS // 2 - 1) as i:
                for u in range(2):
                    step(2 * i + u, u, False, i + 2)
            for j in range(BLOCKS - 3, BLOCKS):
                step(j, j % 2, False, j // 2 + 2)

            turn(2, lambda b, t: XN[:, b, P * t:P * t + P], lambda half: pe.wait_ge(s_xn[2], 4 * half + 4), 0)
            pe.wait_ge(s_tv[2], 4)
            convolve(1)
            back(1)

            turn(3, lambda b, t: XN[:, b, P * t:P * t + P], lambda half: pe.wait_ge(s_xn[3], 4 * half + 4), 0)
            pe.wait_ge(s_tv[3], 4)
            pe.wait_ge(s_in["rw1"], 16)
            for b in range(B):
                for k in range(LT):
                    last = pe.matmul(PS[:, 4 + b // 4, R1 * (b % 4):R1 * (b % 4) + R1], VT[:, k * B + b, :],
                                     RW1[:, k, :], start=k == 0, stop=k == LT - 1)
                if b % 4 == 3:
                    last.then_inc(s_lg1, 1)

            def split_product(dst, high, low, xh, xl, start, stop):
                pe.matmul(dst, high, xh, start=start, stop=False)
                pe.matmul(dst, high, xl, start=False, stop=False)
                return pe.matmul(dst, low, xh, start=False, stop=stop)

            def tok_half(t, k, n):
                return t[:, k * B + 4 * n:k * B + 4 * n + 4, :].rearrange("p b c -> p (b c)")

            pe.wait_ge(s_wsl, 1)
            pe.wait_ge(s_x1, 4)
            for n in range(NT):
                for k in range(LT):
                    w = slice(P * k, P * k + P)
                    last = split_product(bank(2 * n), WSH[:, w], WSL[:, w], tok_half(XH, k, n), tok_half(XL, k, n),
                                         k == 0, k == LT - 1)
                last.then_inc(s_sgu, 1)

            def up(p, u, n, first):
                if n == 0:
                    pe.wait_ge(s_wl[0], p + 1)
                if first:
                    pe.wait_ge(s_ssi, 2 * n + 2)
                else:
                    pe.wait_ge(s_mul, 2 * p + n - 1)
                for g in range(2):
                    for k in range(LT):
                        w = slice(P * (2 * k + g), P * (2 * k + g) + P)
                        last = split_product(bank(2 * n + g), WH[:, u, w], WL[:, u, w], tok_half(XH, k, n),
                                             tok_half(XL, k, n), k == 0, k == LT - 1)
                last.then_inc(s_gu, 1)

            def down(p, u, n, stop=False):
                pe.wait_ge(s_wl[1], p + 1)
                pe.wait_ge(s_lo, 2 * p + n + 1)
                for t in range(LT):
                    w = slice(2 * LT * P + P * t, 2 * LT * P + P * t + P)
                    last = split_product(bank(4 + 2 * t + n), WH[:, u, w], WL[:, u, w], HI[:, n, :], LO[:, n, :],
                                         False, stop)
                last.then_inc(s_dn, 1)

            up(0, 0, 0, True)
            pe.wait_ge(s_w1, 2)
            for b in range(B):
                last = pe.transpose(PS[0:R1, 4 + b // 4, P * (b % 4):P * (b % 4) + P], W1[:, b, :], ident)
                if b % 4 == 3:
                    last.then_inc(s_wt, 1)
            up(0, 0, 1, True)
            pe.wait_ge(s_wts, 2)
            for n in range(NT):
                pe.wait_ge(s_slo, n + 1)
                for t in range(LT):
                    w = slice(LT * P + P * t, LT * P + P * t + P)
                    last = split_product(bank(4 + 2 * t + n), WSH[:, w], WSL[:, w], HI[:, n, :], LO[:, n, :],
                                         True, False)
                last.then_inc(s_sdn, 1)

            def pair(p, u):
                for n in range(NT):
                    up(p, u, n, False)
                    down(p - 1, 1 - u, n)

            with pe.Fori(0, NP1 // 2 - 1) as i:
                for u in range(2):
                    pair(2 * i + u + 1, 1 - u)
            pair(NP1 - 1, 1)
            for n in range(NT):
                down(NP1 - 1, 1, n, True)
            pe.wait_ge(s_acc, 4)
            for q in range(4):
                for k in range(4):
                    b, t = 2 * q + k // 2, k % 2
                    last = pe.transpose(PS[:, q, P * k:P * k + P], OT[:, t * B + b, :], ident)
                last.then_inc(s_fin, 1)


INS = ["x", "ctx", "gates", "skip", "kp0", "kp1", "d1", "rw0", "gu0", "dn0", "sgu0", "sdn0", "rw1", "w1", "ws1", "cst"]


def kernel(**inputs):
    import numpy as np
    import concourse.bacc as bacc
    from concourse.bass_utils import run_bass_kernel_spmd

    a = {k: np.asarray(v) for k, v in inputs.items()}

    def padded(k):
        return np.concatenate([np.zeros((H, PAD), k.dtype), k, np.zeros((H, KP - PAD - L), k.dtype)], 1)

    gu1 = a["L1_ffn_gu_w"].reshape(NP1, 2, 2, I1, LT, P).transpose(0, 5, 4, 2, 1, 3).reshape(NP1, P, 2 * LT * P)
    dn1 = a["L1_ffn_dp_w"].reshape(NP1, 2, L, I1).transpose(0, 1, 3, 2).reshape(NP1, P, L)
    sgu1 = np.concatenate([a["L1_ffn_sh_gate_w"], a["L1_ffn_sh_up_w"]], 0).reshape(P, LT, P).transpose(2, 1, 0)
    sdn1 = np.concatenate([a["L1_ffn_sh_down_w"].T, np.zeros((P - I1, L), np.float32)], 0)
    arrays = {
        "x": a["x"],
        "ctx": a["ctx_2048"],
        "gates": np.stack([a["g_xattn"], a["g_ffn"]], 1).reshape(4),
        "skip": a["fside_S2_0"].reshape(P, 1),
        "kp0": padded(a["L0_xattn_k"]),
        "kp1": padded(a["L1_xattn_ssm_kernel"]),
        "d1": a["L1_xattn_D"].reshape(H, 1),
        "rw0": a["L0_ffn_router_w"],
        "gu0": np.concatenate([a["L0_ffn_gate_w"], a["L0_ffn_up_w"]], 2),
        "dn0": a["L0_ffn_down_w"],
        "sgu0": np.concatenate([a["L0_ffn_shared_gate_w"], a["L0_ffn_shared_up_w"]], 1),
        "sdn0": a["L0_ffn_shared_down_w"],
        "rw1": np.concatenate([a["L1_ffn_gate_w"], a["L1_ffn_sh_gate1_w"]], 0).T,
        "w1": np.concatenate([gu1, dn1], 2),
        "ws1": np.concatenate([sgu1.reshape(P, LT * P), sdn1], 1),
        "cst": shape_constants(),
    }
    nc = bacc.Bacc("TRN2", target_bir_lowering=False, num_devices=1)
    args = []
    for name in INS:
        arrays[name] = np.ascontiguousarray(arrays[name])
        args.append(nc.dram_tensor(name, arrays[name].shape, mybir.dt.from_np(arrays[name].dtype),
                                   kind="ExternalInput").ap())
    args.append(nc.dram_tensor("out", (B, C, L), F32, kind="ExternalOutput").ap())
    gated_layers(nc, *args)
    r = run_bass_kernel_spmd(nc, [arrays], core_ids=[0])
    return r.results[0]["out"]
```

```python
from contextlib import ExitStack

import concourse.bass as bass
from concourse import mybir

P = 128
B, C, L = 8, 128, 256
LT = L // P
HEAD = 8
H = C // HEAD
PAIRS = HEAD * HEAD
PAD = P - 1
KP = 384
E0, F0 = 8, 256
BLOCKS = B * C // P + E0 - 1
SLOTS = BLOCKS * P
E1, I1 = 64, 64
NP1 = E1 // 2
R1 = E1 + 1
GROUP = 4
YBANK = ((0, 2, 0, 2), (2, 4, 6, 0))
YDEEP = (2, 4)
EARLY = 3
TOK = B * C
NT = TOK // 512
WCOLS = LT * 2 * P + L
WPARTS = (slice(0, LT * 2 * P), slice(LT * 2 * P, WCOLS))
EPS = 1e-5

F32 = mybir.dt.float32
F32R = mybir.dt.float32r
BF16 = mybir.dt.bfloat16
I32 = mybir.dt.int32
ALU = mybir.AluOpType
ACT = mybir.ActivationFunctionType
AX = mybir.AxisListType

K_ID, K_LESS, K_HEAD = 0, P, 2 * P
K_FIRST = 3 * P
K_FULL = K_FIRST + E0
K_UPTO = K_FULL + E0 * E0
K_BLOCK = K_UPTO + E0 * E0
K_COLS = K_BLOCK + E0 * BLOCKS


def shape_constants():
    import numpy as np
    k = np.zeros((P, K_COLS), np.float32)
    a = np.arange(P)
    k[:, K_ID:K_ID + P] = np.eye(P)
    k[:, K_LESS:K_LESS + P] = a[:, None] < a[None, :]
    k[:, K_HEAD:K_HEAD + P] = a[:, None] // HEAD == a[None, :] // HEAD
    e = np.arange(E0)
    k[:, K_FIRST:K_FIRST + E0] = E0 - e
    k[:, K_FULL:K_FULL + E0 * E0] = np.tile(P * e, E0)
    k[:, K_UPTO:K_UPTO + E0 * E0] = (e[None, :] <= e[:, None]).reshape(-1)
    k[:, K_BLOCK:K_BLOCK + E0 * BLOCKS] = np.repeat(np.arange(BLOCKS), E0)
    return k


def gated_layers(nc, x, ctx_in, gates, skip, kp0, kp1, d1, rw0, gu0, dn0, sgu0, sdn0, rw1, w1, ws1, cst,
                 out):
    st = ExitStack()
    with st:
        def sb(name, shape, dt=F32):
            return st.enter_context(nc.sbuf_tensor(name, shape, dt))

        def sem(name):
            return st.enter_context(nc.semaphore(name))

        ffn0 = ExitStack()

        def sb0(name, shape, dt=F32):
            return ffn0.enter_context(nc.sbuf_tensor(name, shape, dt))

        kp1d = nc.dram_tensor("kp1d", [H, KP], F32, kind="Internal").ap()
        xsort = nc.dram_tensor("xsort", [SLOTS, L], F32, kind="Internal").ap()
        ysort = nc.dram_tensor("ysort", [SLOTS, L], F32, kind="Internal").ap()
        wtok = nc.dram_tensor("wtok", [R1, TOK], F32, kind="Internal").ap()

        X = sb("X", [P, B, L])
        CN = sb("CN", [P, B, L])
        CR = sb("CR", [P, B, LT, P])
        XN = sb("XN", [P, B, L])
        XS = sb("XS", [P, B, L])
        CT = sb("CT", [P, LT * B, C])
        CRT = sb("CRT", [P, LT * B, C])
        VT = sb("VT", [P, LT * B, C])
        OT = sb("OT", [P, LT * B, C])
        TW = sb("TW", [P, 4, L])
        KV = sb("KV", [P, 2, LT * B * PAIRS])
        Z = sb("Z", [P, 2, LT * B * PAIRS])
        K = sb("K", [P, K_COLS])
        lessb = sb("lessb", [P, P], BF16)
        onesb = sb("onesb", [P, P], BF16)
        skipc = sb("skipc", [P, 1])
        hskip = sb("hskip", [P, P])
        gt = sb("gt", [P, 4])
        gin = sb("gin", [P, 4])
        kpt = sb("kpt", [H, KP])
        dt1 = sb("dt1", [H, 1])
        neghalf = sb("neghalf", [P, B])
        stt = sb("stt", [P, B, 6])
        mv = sb("mv", [P, B, 2])
        ve = sb("ve", [P, B])
        negmean = sb("negmean", [P, B])
        shift = sb("shift", [P, B])
        rstd = sb("rstd", [P, B])
        RW1 = sb("RW1", [P, LT, R1])
        WS = sb("WS", [P, LT * P + L])
        WR = sb("WR", [P, 2, WCOLS])
        RW0 = sb0("RW0", [P, LT, E0])
        GU0 = sb0("GU0", [P, E0, LT, 2 * F0])
        DN0 = sb0("DN0", [P, E0, F0 // P, L])
        SGU0 = sb0("SGU0", [P, LT, 2 * F0])
        SDN0 = sb0("SDN0", [P, F0 // P, L])
        HS = sb0("HS", [P, NT, 2, 512])
        LG = sb0("LG", [P, B, E0])
        eqm = sb0("eqm", [P, B, E0])
        mx = sb0("mx", [P, B])
        pick = sb0("pick", [P, B])
        oh = sb0("oh", [P, B, E0], BF16)
        ex = sb0("ex", [P, B])
        score = sb0("score", [P, B])
        cmpk = sb0("cmpk", [P, E0, E0])
        cnt = sb0("cnt", [P, E0])
        nblk = sb0("nblk", [P, E0])
        upto = sb0("upto", [P, E0])
        start0 = sb0("start0", [P, E0])
        blke = sb0("blke", [1, BLOCKS, E0])
        blkf = sb0("blkf", [1, BLOCKS])
        blki = sb0("blki", [1, BLOCKS], I32)
        slotm = sb0("slotm", [P, B, E0])
        slotf = sb0("slotf", [P, B])
        sloti = sb0("sloti", [P, B], I32)
        zero = sb0("zero", [P, L])
        XB = sb0("XB", [P, 2, L])
        XBT = sb0("XBT", [P, 2, LT, P])
        SG = sb0("SG", [P, 2, F0])
        HB = sb0("HB", [P, 2, F0])
        HBT = sb0("HBT", [P, 2, F0 // P, P])
        YB = sb0("YB", [P, 2, L])

        ffn0.close()
        XH = sb("XH", [P, LT * B, C], F32R)
        XL = sb("XL", [P, LT * B, C], F32R)
        WSH = sb("WSH", [P, LT * P + L], F32R)
        WSL = sb("WSL", [P, LT * P + L], F32R)
        WH = sb("WH", [P, 2, WCOLS], F32R)
        WL = sb("WL", [P, 2, WCOLS], F32R)
        WB = sb("WB", [P, 2, TOK])
        WBS = sb("WBS", [I1, TOK])
        SHS = sb("SHS", [I1, NT, 512])
        SHU = sb("SHU", [I1, NT, 512])
        SI = sb("SI", [P, NT, 512])
        MU = sb("MU", [P, NT, 512])
        TK = sb("TK", [P, NT, 512])
        HI = sb("HI", [P, NT, 512], F32R)
        LO = sb("LO", [P, NT, 512], F32R)
        LG1 = sb("LG1", [P, B, R1])
        top = sb("top", [P, B, 8])
        rest = sb("rest", [P, B, E1])
        keep = sb("keep", [P, B, E1])
        ex1 = sb("ex1", [P, B, E1])
        exs = sb("exs", [P, B])
        den = sb("den", [P, B])
        rden = sb("rden", [P, B])
        W1 = sb("W1", [P, B, R1])
        WTS = sb("WTS", [R1, TOK])

        PS = st.enter_context(nc.psum_tensor("PS", [P, 8, 512], F32))
        ident = K[:, K_ID:K_ID + P]

        s_in = {n: sem("in_" + n) for n in ("x0", "x1", "ctx0", "ctx1", "cst", "small", "kp1", "kp1d", "rw", "sh0", "zero", "rw1", "ws1", "wtok", "wbs",
                                           "out")}
        s_w0 = [sem(f"in_w0_{e}") for e in range(2)]
        s_T = [[sem(f"in_toeplitz{a}_{u}") for u in range(4)] for a in range(2)]
        s_const = sem("constants_made")
        s_d1 = sem("d_added")
        s_dve = sem("vector_steps")
        s_gates = sem("gates_ready")
        s_var = [sem(f"variance{n}") for n in range(4)]
        s_rstd = [sem(f"rstd{n}") for n in range(4)]
        s_xn = [sem(f"normed{n}") for n in range(4)]
        s_rev = sem("ctx_reversed")
        s_tp0 = sem("turned_in_psum0")
        s_tp = [s_tp0] + [sem(f"turned_in_psum{n}") for n in (1, 2, 3)]
        s_tv = [sem(f"turned{n}") for n in range(4)]
        s_ct = sem("ctx_turned")
        s_crt = sem("reversed_ctx_turned")
        s_vc = sem("v_times_ctx")
        s_skip = sem("skip_sums")
        s_kv = [sem(f"kv{a}") for a in range(2)]
        s_conv = [sem(f"conv{a}") for a in range(2)]
        s_z = [sem(f"times_query{a}") for a in range(2)]
        s_red = [sem(f"summed{a}") for a in range(2)]
        s_back = [sem(f"back_in_psum{a}") for a in range(2)]
        s_res = [sem(f"residual{a}") for a in range(2)]
        s_lg = sem("logits0")
        s_mx = sem("best_logit")
        s_ex = sem("exp_best")
        s_oh = sem("onehot")
        s_pos = sem("positions")
        s_slot = sem("slots")
        s_xs = sem("scaled_tokens")
        s_scat = sem("scattered")
        s_shgu = sem("shared_gu")
        s_shsi = sem("shared_silu")
        s_shh = sem("shared_hidden")
        s_shdn = sem("shared_down")
        s_shadd = sem("shared_added")
        s_bx = sem("block_turned_psum")
        s_bxt = sem("block_turned")
        s_bgu = sem("block_gu")
        s_bsi = sem("block_silu")
        s_bh = sem("block_hidden")
        s_bhp = sem("block_hidden_psum")
        s_bht = sem("block_hidden_turned")
        s_bdn = sem("block_down")
        s_by = sem("block_y")
        s_byo = [sem(f"block_stored{i}") for i in range(2)]
        s_xb = [sem(f"in_block{i}") for i in range(2)]
        s_yg = [sem(f"gathered{b}") for b in range(B)]
        s_raw = [sem(f"in_raw{i}") for i in range(2)]
        s_wb = [sem(f"in_weights_of_tokens{i}") for i in range(2)]
        s_x1 = sem("x_split")
        s_lg1 = sem("logits1")
        s_e1 = sem("exp_in")
        s_ee = sem("exp_out")
        s_w1 = sem("token_weights")
        s_wt = sem("token_weights_psum")
        s_wts = sem("token_weights_turned")
        s_wsh = sem("shared1_high")
        s_wsl = sem("shared1_low")
        s_sgu = sem("shared1_gu")
        s_ssi = sem("shared1_silu")
        s_stw = sem("shared1_weighted")
        s_shi = sem("shared1_hi")
        s_slo = sem("shared1_lo")
        s_sdn = sem("shared1_down")
        s_wh = [sem("pair_high_up"), sem("pair_high_down")]
        s_wl = [sem("pair_low_up"), sem("pair_low_down")]
        s_gu = sem("pair_gu")
        s_si = sem("pair_silu")
        s_mul = sem("pair_product")
        s_zero1 = sem("upper_rows_zeroed")
        s_tw = sem("pair_weighted")
        s_hi = sem("pair_hi")
        s_lo = sem("pair_lo")
        s_dn = sem("pair_down")
        s_acc = [sem(f"sum_out_of_psum{t}") for t in range(LT)]
        s_fin = sem("final_psum")
        s_end = sem("final")
        block = st.enter_context(nc.Block())

        x_n = x.rearrange("b c l -> c b l")
        c_n = ctx_in.rearrange("b c l -> c b l")
        out_n = out.rearrange("b c l -> c b l")

        def bank(i, n=512):
            return PS[:, i, 0:n]

        def head(t, h):
            return t[:, :, bass.ds(HEAD * h, HEAD)]

        def over_j(ap):
            return ap.unsqueeze(3).broadcast_to([P, LT * B, HEAD, HEAD])

        def over_i(ap):
            return ap.unsqueeze(2).broadcast_to([P, LT * B, HEAD, HEAD])

        def pairs(ap):
            return ap.rearrange("p (a i j) -> p a i j", i=HEAD, j=HEAD)

        @block.sync
        def _(sp):
            for name, dst, src in (("x", X, x_n), ("ctx", CN, c_n)):
                for half in range(2):
                    b = slice(4 * half, 4 * half + 4)
                    sp.dma_start(dst[:, b, :], src[:, b, :]).then_inc(s_in[name + str(half)], 16)

            def toeplitz(a, kp, h, u):
                rows = bass.AP(tensor=kp.tensor, offset=0, ap=[[KP, H], [1, P], [1, L]])
                sp.dma_start(TW[:, u:u + 1, :], rows[bass.ds(h, 1), :, :].rearrange("o p l -> p o l")
                             ).then_inc(s_T[a][u], 16)

            for a, kp in ((0, kp0), (1, kp1d)):
                if a:
                    sp.wait_ge(s_in["kp1d"], 16)
                for u in range(4):
                    if a:
                        sp.wait_ge(s_conv[0], H)
                    toeplitz(a, kp, u, u)
                with sp.Fori(1, H // GROUP) as i:
                    for u in range(4):
                        sp.wait_ge(s_conv[a], GROUP * i + (u - 3))
                        toeplitz(a, kp, GROUP * i + u, u)
                if a == 0:
                    sp.wait_ge(s_scat, 16 * B)
                    xs_r = xsort.rearrange("(j p) l -> p j l", p=P)

                    def load_x(j, par):
                        sp.dma_start(XB[:, par:par + 1, :], xs_r[:, bass.ds(j, 1), :]).then_inc(s_xb[par], 16)

                    def step(j, par):
                        sp.wait_ge(s_bx, j + 1)
                        load_x(j + 2, par)

                    load_x(0, 0)
                    load_x(1, 1)
                    with sp.Fori(0, BLOCKS // 2 - 1) as i:
                        for par in range(2):
                            step(2 * i + par, par)
                    step(BLOCKS - 3, 0)

            def raw(p, u):
                sp.dma_start(WR[:, u:u + 1, :], w1[bass.ds(p, 1), :, :].rearrange("o p n -> p o n")
                             ).then_inc(s_raw[u], 16)

            def token_weights(p, u):
                rows = bass.AP(tensor=wtok.tensor, offset=0, ap=[[TOK, R1], [0, I1], [1, TOK]])
                for e in range(2):
                    sp.dma_start(WB[I1 * e:I1 * e + I1, u:u + 1, :],
                                 rows[bass.ds(2 * p + e, 1), :, :].rearrange("o p t -> p o t")
                                 ).then_inc(s_wb[u], 16)

            def raw_again(p, u):
                for part in range(2):
                    sp.wait_ge(s_wl[part], p - 1)
                raw(p, u)

            def token_weights_again(p, u):
                sp.wait_ge(s_tw, 2 * p - 2)
                token_weights(p, u)

            for u in range(2):
                raw(u, u)
            for u in range(2):
                raw_again(2 + u, u)
            sp.wait_ge(s_in["wtok"], 16)
            sp.dma_start(WBS[:, :], wtok[E1:E1 + 1, :].partition_broadcast(I1)).then_inc(s_in["wbs"], 16)
            for u in range(2):
                token_weights(u, u)
            with sp.Fori(1, NP1 // 2 - 1) as i:
                for u in range(2):
                    token_weights_again(2 * i + u, u)
                    raw_again(2 * i + 2 + u, u)
            for u in range(2):
                token_weights_again(NP1 - 2 + u, u)
            for q in range(4):
                sp.wait_ge(s_end, q + 1)
                sp.dma_start(out_n[:, 2 * q:2 * q + 2, :], X[:, 2 * q:2 * q + 2, :]).then_inc(s_in["out"], 16)
            sp.wait_ge(s_in["out"], 64)

        @block.gpsimd
        def _(pool):
            pool.memset(neghalf[:], -0.5).then_inc(s_const, 1)
            pool.memset(onesb[:], 1.0).then_inc(s_const, 1)
            pool.memset(zero[:], 0.0).then_inc(s_const, 1)

            def rstd_of(n, between=None):
                for half in range(2):
                    if half and between:
                        between()
                    b = slice(4 * half, 4 * half + 4)
                    pool.wait_ge(s_const, 1)
                    pool.wait_ge(s_var[n], half + 1)
                    if n:
                        pool.wait_ge(s_xn[n - 1], B)
                    pool.tensor_tensor(rstd[:, b], ve[:, b], neghalf[:, b], ALU.pow).then_inc(s_rstd[n], 1)
                    pool.wait_ge(s_rstd[n], 2 * half + 1)
                    pool.tensor_tensor(shift[:, b], negmean[:, b], rstd[:, b], ALU.mult).then_inc(s_rstd[n], 1)

            def product(a, left, right, h, u, first):
                if not first:
                    pool.wait_ge(s_conv[a], h - 1)
                pool.tensor_tensor(pairs(KV[:, u % 2, :]), over_j(head(left, h)), over_i(head(right, h)),
                                   ALU.mult).then_inc(s_kv[a], 1)

            def products(a, left, right, done):
                for u in range(done, GROUP):
                    product(a, left, right, u, u, u < 2)
                with pool.Fori(1, H // GROUP) as i:
                    for u in range(GROUP):
                        product(a, left, right, GROUP * i + u, u, False)

            rstd_of(0)
            pool.wait_ge(s_tv[0], 4)
            pool.wait_ge(s_crt, 4)
            products(0, VT, CRT, 0)
            rstd_of(1)
            pool.wait_ge(s_slot, 2)
            pool.wait_ge(s_in["zero"], 16)
            for b in range(B):
                pool.wait_ge(s_xs, b + 1)
                pool.indirect_dma_start(out=xsort, out_offset=bass.IndirectOffsetOnAxis(ap=sloti[:, b:b + 1], axis=0),
                                        in_=XS[:, b, :], in_offset=None).then_inc(s_scat, 16)
            pool.wait_ge(s_conv[0], H)
            for u in range(2):
                product(1, CRT, CRT, u, u, True)
            ys_r = ysort.rearrange("(j p) l -> p j l", p=P)

            def store_y(j, par):
                pool.wait_ge(s_by, j + 1)
                pool.dma_start(ys_r[:, bass.ds(j, 1), :], YB[:, par:par + 1, :]).then_inc(s_byo[par], 16)

            with pool.Fori(0, BLOCKS // 2) as i:
                for par in range(2):
                    store_y(2 * i + par, par)
            store_y(BLOCKS - 1, 0)
            pool.wait_ge(s_byo[0], 16 * ((BLOCKS + 1) // 2))
            pool.wait_ge(s_byo[1], 16 * (BLOCKS // 2))
            pool.wait_ge(s_scat, 16 * B)
            for b in range(B):
                pool.indirect_dma_start(out=XS[:, b, :], out_offset=None, in_=ysort,
                                        in_offset=bass.IndirectOffsetOnAxis(ap=sloti[:, b:b + 1], axis=0)
                                        ).then_inc(s_yg[b], 16)
            rstd_of(2, lambda: product(1, CRT, CRT, 2, 2, False))
            products(1, CRT, CRT, EARLY)
            pool.memset(HI[:, :, :].bitcast(F32), 0.0).then_inc(s_zero1, 1)
            pool.memset(LO[:, :, :].bitcast(F32), 0.0).then_inc(s_zero1, 1)
            rstd_of(3)
            pool.wait_ge(s_wsh, 1)
            pool.tensor_tensor(WSL[:, :], WS[:, :], WSH[:, :].bitcast(F32), ALU.subtract).then_inc(s_wsl, 1)
            with pool.Fori(0, NP1 // 2) as i:
                for u in range(2):
                    for part in range(2):
                        pool.wait_ge(s_wh[part], 2 * i + u + 1)
                        w = WPARTS[part]
                        pool.tensor_tensor(WL[:, u, w], WR[:, u, w], WH[:, u, w].bitcast(F32), ALU.subtract
                                           ).then_inc(s_wl[part], 1)

        @block.scalar
        def _(act):
            act.dma_start(K[:, :], cst).then_inc(s_in["cst"], 16)
            act.dma_start(gin[:, :], gates.partition_broadcast(P)).then_inc(s_in["small"], 16)
            act.dma_start(skipc[:, :], skip).then_inc(s_in["small"], 16)
            act.dma_start(kpt[:, :], kp1).then_inc(s_in["kp1"], 16)
            act.dma_start(dt1[:, :], d1).then_inc(s_in["kp1"], 16)

            def normed(n, dst):
                for half in range(2):
                    act.wait_ge(s_rstd[n], 2 * half + 2)
                    for b in range(4 * half, 4 * half + 4):
                        act.activation(dst(b), X[:, b, :].rearrange("c (t m) -> c t m", t=LT), ACT.Identity,
                                       scale=rstd[:, b:b + 1], bias=shift[:, b:b + 1]).then_inc(s_xn[n], 1)

            def forward(b):
                return XN[:, b, :].rearrange("c (t m) -> c t m", t=LT)

            normed(0, lambda b: forward(b)[:, :, ::-1])
            for half in range(2):
                act.wait_ge(s_in["ctx" + str(half)], 16)
                b = slice(4 * half, 4 * half + 4)
                act.activation(CR[:, b, :, :], CN[:, b, :].rearrange("c b (t m) -> c b t m", t=LT)[:, :, :, ::-1],
                               ACT.Copy).then_inc(s_rev, 1)

            def out_of_psum(n, dst, first, base, done):
                for q in range(4):
                    act.wait_ge(s_tp[n], first + q + 1)
                    t, half = q % 2, q // 2
                    act.activation(dst[:, t * B + 4 * half:t * B + 4 * half + 4, :],
                                   PS[:, base + q, :].rearrange("p (b c) -> p b c", b=4), ACT.Copy
                                   ).then_inc(done, 1)

            out_of_psum(0, CRT, 8, 0, s_crt)
            act.wait_ge(s_in["cst"], 16)
            act.activation(lessb[:, :], K[:, K_LESS:K_LESS + P], ACT.Copy).then_inc(s_rev, 1)
            act.wait_ge(s_in["small"], 32)
            act.activation(gt[:, :], gin[:, :], ACT.Tanh).then_inc(s_gates, 1)
            act.dma_start(RW0[:, :, :], rw0.rearrange("(k p) e -> p k e", p=P)).then_inc(s_in["rw"], 16)
            act.dma_start(SGU0[:, :, :], sgu0.rearrange("(k p) f -> p k f", p=P)).then_inc(s_in["sh0"], 16)
            act.dma_start(SDN0[:, :, :], sdn0.rearrange("(k p) f -> p k f", p=P)).then_inc(s_in["sh0"], 16)
            act.wait_ge(s_const, 3)
            act.dma_start(xsort.rearrange("(j p) l -> p j l", p=P),
                          zero[:].unsqueeze(1).broadcast_to([P, BLOCKS, L])).then_inc(s_in["zero"], 16)
            for e in range(E0):
                act.wait_ge(s_conv[0], e + 1)
                act.dma_start(GU0[:, e, :, :], gu0[e].rearrange("(k p) f -> p k f", p=P)).then_inc(s_w0[0], 16)
                act.dma_start(DN0[:, e, :, :], dn0[e].rearrange("(k p) f -> p k f", p=P)).then_inc(s_w0[1], 16)
            act.wait_ge(s_d1, 1)
            act.dma_start(kp1d, kpt[:, :]).then_inc(s_in["kp1d"], 16)
            act.dma_start(RW1[:, :, :], rw1.rearrange("(k p) e -> p k e", p=P)).then_inc(s_in["rw1"], 16)
            act.dma_start(WS[:, :], ws1).then_inc(s_in["ws1"], 16)
            normed(1, forward)
            act.wait_ge(s_mx, 1)
            act.activation(ex[:, :], mx[:, :], ACT.Exp, scale=-1.0).then_inc(s_ex, 1)
            for n in range(2):
                act.wait_ge(s_shgu, n + 1)
                for f in range(2):
                    act.activation(HS[:, n, f, :], bank(f), ACT.Silu).then_inc(s_shsi, 1)

            def turn_block(j, par, first):
                act.wait_ge(s_bx, j + 1)
                if not first:
                    act.wait_ge(s_bgu, j - 1)
                act.activation(XBT[:, par, :, :], PS[:, par, 0:L].rearrange("p (k s) -> p k s", k=LT), ACT.Copy
                               ).then_inc(s_bxt, 1)

            def silu_block(j, par, first):
                act.wait_ge(s_bgu, j + 1)
                if not first:
                    act.wait_ge(s_bh, j - 1)
                act.activation(SG[:, par, :], PS[:, 4 + par, 0:F0], ACT.Silu).then_inc(s_bsi, 1)

            turn_block(0, 0, True)
            silu_block(0, 0, True)
            turn_block(1, 1, True)

            def step(i, u, first):
                j = 2 * i + u
                silu_block(j + 1, 1 - u, first and u == 0)
                turn_block(j + 2, u, False)
                act.wait_ge(s_bdn, j + 1)
                if not first:
                    act.wait_ge(s_byo[u], 16 * i)
                act.activation(YB[:, u, :], PS[:, 6 + u, 0:L], ACT.Copy).then_inc(s_by, 1)

            for u in range(2):
                step(0, u, True)
            with act.Fori(1, BLOCKS // 2 - 1) as i:
                for u in range(2):
                    step(i, u, False)
            for j in range(BLOCKS - 3, BLOCKS):
                if j + 1 < BLOCKS:
                    silu_block(j + 1, (j + 1) % 2, False)
                if j + 2 < BLOCKS:
                    turn_block(j + 2, j % 2, False)
                act.wait_ge(s_bdn, j + 1)
                act.wait_ge(s_byo[j % 2], 16 * (j // 2))
                act.activation(YB[:, j % 2, :], PS[:, 6 + j % 2, 0:L], ACT.Copy).then_inc(s_by, 1)

            normed(2, forward)

            normed(3, forward)
            out_of_psum(3, VT, 0, 0, s_tv[3])

            def high(part, p, u, first):
                act.wait_ge(s_raw[u], 16 * (p // 2 + 1) if isinstance(p, int) else first)
                if not isinstance(p, int) or p >= 2:
                    act.wait_ge((s_gu, s_dn)[part], 2 * p - 2)
                w = WPARTS[part]
                act.activation(WH[:, u, w], WR[:, u, w], ACT.Copy).then_inc(s_wh[part], 1)

            act.wait_ge(s_in["ws1"], 16)
            act.activation(WSH[:, :], WS[:, :], ACT.Copy).then_inc(s_wsh, 1)
            for p in range(2):
                for part in range(2):
                    high(part, p, p, None)
            act.wait_ge(s_e1, 1)
            act.activation(ex1[:, :, :], ex1[:, :, :], ACT.Exp).then_inc(s_ee, 1)
            act.activation(exs[:, :], LG1[:, :, E1], ACT.Exp, scale=-1.0).then_inc(s_ee, 1)
            for n in range(NT):
                act.wait_ge(s_sgu, n + 1)
                act.activation(SHS[:, n, :], PS[0:I1, 6 + n, :], ACT.Silu).then_inc(s_ssi, 1)
                act.activation(SHU[:, n, :], PS[I1:P, 6 + n, :], ACT.Copy).then_inc(s_ssi, 1)

            def silu(p, n, first):
                act.wait_ge(s_gu, 2 * p + n + 1)
                if not first:
                    act.wait_ge(s_mul, 2 * p + n - 1)
                act.activation(SI[:, n, :], bank(2 * n), ACT.Silu).then_inc(s_si, 1)

            def hidden_high(p, n, first):
                act.wait_ge(s_tw, 2 * p + n + 1)
                if first:
                    act.wait_ge(s_sdn, n + 1)
                else:
                    act.wait_ge(s_dn, 2 * p + n - 1)
                act.activation(HI[:, n, :], TK[:, n, :], ACT.Copy).then_inc(s_hi, 1)

            silu(0, 0, True)
            for n in range(2):
                act.wait_ge(s_wt, n + 1)
                act.activation(WTS[:, 512 * n:512 * n + 512], PS[0:R1, 4 + n, :], ACT.Copy).then_inc(s_wts, 1)
            act.wait_ge(s_wts, 2)
            act.dma_start(wtok, WTS[:, :]).then_inc(s_in["wtok"], 16)
            silu(0, 1, True)
            silu(1, 0, False)
            high(0, 2, 0, None)
            silu(1, 1, False)
            act.wait_ge(s_zero1, 1)
            for n in range(NT):
                act.wait_ge(s_stw, n + 1)
                act.activation(HI[0:I1, n, :], SHU[:, n, :], ACT.Copy).then_inc(s_shi, 1)
            for n in range(NT):
                hidden_high(0, n, True)
            hidden_high(1, 0, False)
            high(1, 2, 0, None)
            hidden_high(1, 1, False)

            def pair(p, u, more, nxt):
                for n in range(NT):
                    silu(p, n, False)
                    if n == 0 and more:
                        high(0, p + 1, 1 - u, nxt)
                    hidden_high(p, n, False)
                    if n == 1 and more:
                        high(1, p + 1, 1 - u, nxt)

            with act.Fori(1, NP1 // 2 - 1) as i:
                pair(2 * i, 0, True, 16 * (i + 1))
                pair(2 * i + 1, 1, True, 16 * (i + 2))
            pair(NP1 - 2, 0, True, None)
            pair(NP1 - 1, 1, False, None)
            for n in range(NT):
                act.wait_ge(s_dn, 2 * NP1 - 1 + n)
                act.activation(OT[:, 4 * n:4 * n + 4, :].rearrange("p b c -> p (b c)"), bank(4 + n), ACT.Copy
                               ).then_inc(s_acc[0], 1)

        @block.vector
        def _(dve):
            n_own = [0]

            def own(ins):
                n_own[0] += 1
                ins.then_inc(s_dve, 1)

            def settle():
                dve.wait_ge(s_dve, n_own[0])

            def norm_stats(n, before):
                for half in range(2):
                    before(half)
                    for b in range(4 * half, 4 * half + 4):
                        own(dve.bn_stats(stt[:, b, :], X[:, b, :]))
                    settle()
                    for b in range(4 * half, 4 * half + 4):
                        own(dve.bn_aggr(mv[:, b, :], stt[:, b, :]))
                    settle()
                    b = slice(4 * half, 4 * half + 4)
                    if n:
                        dve.wait_ge(s_rstd[n - 1], 4)
                    own(dve.tensor_scalar(negmean[:, b], mv[:, b, 0], -1.0, None, ALU.mult))
                    dve.tensor_scalar_add(ve[:, b], mv[:, b, 1], EPS).then_inc(s_var[n], 1)
                    settle()

            def out_of_psum(n, dst, first, base, done, banks=4):
                for q in range(4):
                    dve.wait_ge(s_tp[n], first + q + 1)
                    t, half = q % 2, q // 2
                    dve.tensor_copy(dst[:, t * B + 4 * half:t * B + 4 * half + 4, :],
                                    PS[:, base + q % banks, :].rearrange("p (b c) -> p b c", b=4)).then_inc(done, 1)

            norm_stats(0, lambda half: dve.wait_ge(s_in["x" + str(half)], 16))
            out_of_psum(0, VT, 0, 0, s_tv[0])
            out_of_psum(0, CT, 4, 4, s_ct)
            dve.wait_ge(s_in["kp1"], 32)
            dve.tensor_tensor(kpt[:, PAD:PAD + 1], kpt[:, PAD:PAD + 1], dt1[:, :], ALU.add).then_inc(s_d1, 1)
            dve.wait_ge(s_in["cst"], 16)
            dve.wait_ge(s_in["small"], 32)
            dve.wait_ge(s_rev, 2)
            dve.wait_ge(s_xn[0], B)
            own(dve.tensor_scalar(hskip[:, :], K[:, K_HEAD:K_HEAD + P], skipc[:, 0:1], None, ALU.mult))
            CRf = CR[:, :, :, :].rearrange("c b t m -> c b (t m)")
            dve.tensor_tensor(XS[:, :, :], XN[:, :, :], CRf, ALU.mult).then_inc(s_vc, 1)
            dve.wait_ge(s_gates, 1)
            for q in range(4):
                b = slice(2 * q, 2 * q + 2)
                dve.wait_ge(s_skip, q + 1)
                own(dve.tensor_tensor(XS[:, b, :], bank(4 + q).rearrange("c (b l) -> c b l", b=2), CRf[:, b, :],
                                      ALU.mult))
            settle()
            for b in range(B):
                own(dve.scalar_tensor_tensor(
                    X[:, b, :].rearrange("c (t m) -> c t m", t=LT),
                    XS[:, b, :].rearrange("c (t m) -> c t m", t=LT)[:, :, ::-1], gt[:, 0:1],
                    X[:, b, :].rearrange("c (t m) -> c t m", t=LT), ALU.mult, ALU.add))

            def combine(a, query):
                def times_query(h, u, first):
                    dve.wait_ge(s_conv[a], h + 1)
                    if not first:
                        dve.wait_ge(s_red[a], h - 1)
                    y = PS[:, YBANK[a][u]:YBANK[a][u] + 2, :].rearrange("p t n -> p (t n)")
                    dve.tensor_tensor(pairs(Z[:, u % 2, :]), pairs(y), over_j(head(query, h)), ALU.mult
                                      ).then_inc(s_z[a], 1)

                def sums(h, u):
                    dve.wait_ge(s_z[a], h + 1)
                    dve.tensor_reduce(head(OT, h), pairs(Z[:, u % 2, :]).rearrange("p a i j -> p a j i"), AX.X,
                                      ALU.add).then_inc(s_red[a], 1)

                times_query(0, 0, True)
                times_query(1, 1, True)
                sums(0, 0)
                for u in range(2, GROUP):
                    times_query(u, u, False)
                    sums(u - 1, u - 1)
                with dve.Fori(1, H // GROUP) as i:
                    for u in range(GROUP):
                        times_query(GROUP * i + u, u, False)
                        sums(GROUP * i + u - 1, (u - 1) % GROUP)
                sums(H - 1, GROUP - 1)

            def add_back(a, g, half):
                for q in range(2 * half, 2 * half + 2):
                    dve.wait_ge(s_back[a], q + 1)
                    own(dve.scalar_tensor_tensor(X[:, 2 * q:2 * q + 2, :].rearrange("c b l -> c (b l)"), bank(4 + q),
                                                 g, X[:, 2 * q:2 * q + 2, :].rearrange("c b l -> c (b l)"),
                                                 ALU.mult, ALU.add))
                settle()

            dve.wait_ge(s_ct, 4)
            settle()
            combine(0, CT)

            norm_stats(1, lambda half: add_back(0, gt[:, 0:1], half))
            dve.wait_ge(s_kv[0], H)
            out_of_psum(1, VT, 0, 0, s_tv[1])
            dve.wait_ge(s_lg, 1)
            own(dve.tensor_copy(LG[:, :, :], PS[:, 4, 0:B * E0].rearrange("p (b e) -> p b e", b=B)))
            settle()
            dve.tensor_reduce(mx[:, :], LG[:, :, :], AX.X, ALU.max).then_inc(s_mx, 1)
            dve.wait_ge(s_mx, 1)
            own(dve.tensor_tensor(eqm[:, :, :], LG[:, :, :], mx[:].unsqueeze(2).broadcast_to([P, B, E0]),
                                  ALU.is_equal))
            settle()
            own(dve.tensor_tensor(LG[:, :, :], eqm[:, :, :],
                                  K[:, K_FIRST:K_FIRST + E0].unsqueeze(1).broadcast_to([P, B, E0]), ALU.mult))
            settle()
            own(dve.tensor_reduce(pick[:, :], LG[:, :, :], AX.X, ALU.max))
            settle()
            dve.tensor_tensor(oh[:, :, :], LG[:, :, :], pick[:].unsqueeze(2).broadcast_to([P, B, E0]),
                              ALU.is_equal).then_inc(s_oh, 1)
            dve.wait_ge(s_ex, 1)
            own(dve.tensor_scalar_add(ex[:, :], ex[:, :], 1.0))
            settle()
            own(dve.reciprocal(score[:, :], ex[:, :]))
            settle()
            dve.wait_ge(s_xn[1], B)
            for b in range(B):
                dve.tensor_scalar(XS[:, b, :], XN[:, b, :], score[:, b:b + 1], None, ALU.mult).then_inc(s_xs, 1)
            dve.wait_ge(s_pos, 1)
            own(dve.tensor_reduce(cnt[:, :], PS[:, 5, B * E0:2 * B * E0].rearrange("p (b e) -> p e b", b=B), AX.X,
                                  ALU.add))
            settle()
            own(dve.tensor_tensor(cmpk[:, :, :], cnt[:].unsqueeze(2).broadcast_to([P, E0, E0]),
                                  K[:, K_FULL:K_FULL + E0 * E0].rearrange("p (e k) -> p e k", e=E0), ALU.is_gt))
            settle()
            own(dve.tensor_reduce(nblk[:, :], cmpk[:, :, :], AX.X, ALU.add))
            settle()
            own(dve.tensor_tensor(cmpk[:, :, :], nblk[:].unsqueeze(1).broadcast_to([P, E0, E0]),
                                  K[:, K_UPTO:K_UPTO + E0 * E0].rearrange("p (e k) -> p e k", e=E0), ALU.mult))
            settle()
            own(dve.tensor_reduce(upto[:, :], cmpk[:, :, :], AX.X, ALU.add))
            settle()
            own(dve.tensor_tensor(start0[:, :], upto[:, :], nblk[:, :], ALU.subtract))
            settle()
            own(dve.tensor_scalar(start0[:, :], start0[:, :], float(P), None, ALU.mult))
            settle()
            own(dve.tensor_tensor(slotm[:, :, :], PS[:, 5, 0:B * E0].rearrange("p (b e) -> p b e", b=B),
                                  start0[:].unsqueeze(1).broadcast_to([P, B, E0]), ALU.add))
            settle()
            own(dve.tensor_tensor(slotm[:, :, :], slotm[:, :, :], oh[:, :, :], ALU.mult))
            settle()
            own(dve.tensor_reduce(slotf[:, :], slotm[:, :, :], AX.X, ALU.add))
            settle()
            dve.tensor_copy(sloti[:, :], slotf[:, :]).then_inc(s_slot, 1)
            own(dve.tensor_tensor(blke[:, :, :], upto[0:1, :].unsqueeze(1).broadcast_to([1, BLOCKS, E0]),
                                  K[0:1, K_BLOCK:K_BLOCK + E0 * BLOCKS].rearrange("p (j e) -> p j e", e=E0),
                                  ALU.is_le))
            settle()
            own(dve.tensor_reduce(blkf[:, :], blke[:, :, :], AX.X, ALU.add))
            settle()
            own(dve.tensor_scalar_min(blkf[:, :], blkf[:, :], float(E0 - 1)))
            settle()
            dve.tensor_copy(blki[:, :], blkf[:, :]).then_inc(s_slot, 1)
            for n in range(2):
                for f in range(2):
                    dve.wait_ge(s_shsi, 2 * n + f + 1)
                    dve.tensor_tensor(HS[:, n, f, :], HS[:, n, f, :], bank(2 + f), ALU.mult).then_inc(s_shh, 1)

            def hidden(i, u, first, j=None):
                j = 2 * i + u if j is None else j
                dve.wait_ge(s_bsi, j + 1)
                if not first:
                    dve.wait_ge(s_bhp, j - 1)
                dve.tensor_tensor(HB[:, u, :], SG[:, u, :], PS[:, 4 + u, F0:2 * F0], ALU.mult).then_inc(s_bh, 1)
                dve.wait_ge(s_bhp, j + 1)
                if not first:
                    dve.wait_ge(s_bdn, j - 1)
                dve.tensor_copy(HBT[:, u, :, :], PS[:, 2 + u, 0:F0].rearrange("p (k s) -> p k s", k=F0 // P)
                                ).then_inc(s_bht, 1)

            for u in range(2):
                hidden(0, u, True)
            with dve.Fori(1, BLOCKS // 2) as i:
                for u in range(2):
                    hidden(i, u, False)
            hidden(0, (BLOCKS - 1) % 2, False, BLOCKS - 1)

            for q in range(4):
                dve.wait_ge(s_shdn, q // 2 + 1)
                b = slice(2 * q, 2 * q + 2)
                dve.scalar_tensor_tensor(X[:, b, :].rearrange("c b l -> c (b l)"), bank(q), gt[:, 1:2],
                                         X[:, b, :].rearrange("c b l -> c (b l)"), ALU.mult, ALU.add
                                         ).then_inc(s_shadd, 1)

            def gathered(half):
                dve.wait_ge(s_shadd, 4)
                for b in range(4 * half, 4 * half + 4):
                    dve.wait_ge(s_yg[b], 16)
                    own(dve.scalar_tensor_tensor(X[:, b, :], XS[:, b, :], gt[:, 1:2], X[:, b, :], ALU.mult, ALU.add))
                settle()

            norm_stats(2, gathered)
            out_of_psum(2, VT, 0, 0, s_tv[2], 2)
            dve.wait_ge(s_tv[2], 4)
            dve.wait_ge(s_red[0], H)
            combine(1, VT)

            norm_stats(3, lambda half: add_back(1, gt[:, 2:3], half))
            for q in range(4):
                dve.wait_ge(s_tv[3], q + 1)
                part = slice((q % 2) * B + 4 * (q // 2), (q % 2) * B + 4 * (q // 2) + 4)
                own(dve.tensor_copy(XH[:, part, :], VT[:, part, :]))
                settle()
                dve.tensor_tensor(XL[:, part, :], VT[:, part, :], XH[:, part, :].bitcast(F32), ALU.subtract
                                  ).then_inc(s_x1, 1)
            for n in range(2):
                dve.wait_ge(s_lg1, n + 1)
                own(dve.tensor_copy(LG1[:, 4 * n:4 * n + 4, :],
                                    PS[:, 4 + n, 0:4 * R1].rearrange("p (b e) -> p b e", b=4)))
            settle()
            for b in range(B):
                own(dve.max(top[:, b, :], LG1[:, b, 0:E1]))
            settle()
            dve.tensor_tensor(ex1[:, :, :], LG1[:, :, 0:E1], top[:, :, 0:1].broadcast_to([P, B, E1]), ALU.subtract
                              ).then_inc(s_e1, 1)
            for b in range(B):
                own(dve.match_replace(rest[:, b, :], top[:, b, :], LG1[:, b, 0:E1], -3.0e38))
            settle()
            own(dve.tensor_tensor(keep[:, :, :], rest[:, :, :], LG1[:, :, 0:E1], ALU.not_equal))
            settle()
            dve.wait_ge(s_ee, 2)
            own(dve.tensor_tensor(keep[:, :, :], keep[:, :, :], ex1[:, :, :], ALU.mult))
            own(dve.tensor_scalar_add(exs[:, :], exs[:, :], 1.0))
            settle()
            own(dve.tensor_reduce(den[:, :], keep[:, :, :], AX.X, ALU.add))
            settle()
            own(dve.reciprocal(rden[:, :], den[:, :]))
            settle()
            dve.tensor_tensor(W1[:, :, 0:E1], keep[:, :, :], rden[:].unsqueeze(2).broadcast_to([P, B, E1]), ALU.mult
                              ).then_inc(s_w1, 1)
            dve.reciprocal(W1[:, :, E1], exs[:, :]).then_inc(s_w1, 1)

            def product(p, n, first):
                dve.wait_ge(s_si, 2 * p + n + 1)
                if not first:
                    dve.wait_ge(s_tw, 2 * p + n - 1)
                dve.tensor_tensor(MU[:, n, :], SI[:, n, :], bank(2 * n + 1), ALU.mult).then_inc(s_mul, 1)

            def weighted(p, u, n, rounds):
                dve.wait_ge(s_wb[u], 32 * rounds)
                dve.wait_ge(s_mul, 2 * p + n + 1)
                dve.tensor_tensor(TK[:, n, :], MU[:, n, :], WB[:, u, 512 * n:512 * n + 512], ALU.mult
                                  ).then_inc(s_tw, 1)

            def hidden_low(p, n):
                dve.wait_ge(s_hi, 2 * p + n + 1)
                dve.tensor_tensor(LO[:, n, :], TK[:, n, :], HI[:, n, :].bitcast(F32), ALU.subtract
                                  ).then_inc(s_lo, 1)

            for n in range(NT):
                dve.wait_ge(s_ssi, 2 * n + 2)
                own(dve.tensor_tensor(SHU[:, n, :], SHS[:, n, :], SHU[:, n, :], ALU.mult))
            product(0, 0, True)
            product(0, 1, True)
            settle()
            dve.wait_ge(s_in["wbs"], 16)
            for n in range(NT):
                dve.tensor_tensor(SHU[:, n, :], SHU[:, n, :], WBS[:, 512 * n:512 * n + 512], ALU.mult
                                  ).then_inc(s_stw, 1)
            dve.wait_ge(s_zero1, 2)
            for n in range(NT):
                dve.wait_ge(s_shi, n + 1)
                dve.tensor_tensor(LO[0:I1, n, :], SHU[:, n, :], HI[0:I1, n, :].bitcast(F32), ALU.subtract
                                  ).then_inc(s_slo, 1)
            for n in range(NT):
                weighted(0, 0, n, 1)
            dve.wait_ge(s_slo, 2)
            for n in range(NT):
                hidden_low(0, n)
            for n in range(NT):
                product(1, n, False)
                dve.wait_ge(s_lo, n + 1)
                weighted(1, 1, n, 1)
                hidden_low(1, n)

            with dve.Fori(1, NP1 // 2) as i:
                for u in range(2):
                    for n in range(NT):
                        product(2 * i + u, n, False)
                        weighted(2 * i + u, u, n, i + 1)
                        hidden_low(2 * i + u, n)
            for n in range(NT):
                dve.wait_ge(s_dn, 2 * NP1 - 1 + n)
                dve.tensor_copy(OT[:, B + 4 * n:B + 4 * n + 4, :].rearrange("p b c -> p (b c)"), bank(6 + n)
                                ).then_inc(s_acc[1], 1)
            for q in range(4):
                dve.wait_ge(s_fin, q + 1)
                xq = X[:, 2 * q:2 * q + 2, :].rearrange("c b l -> c (b l)")
                dve.scalar_tensor_tensor(xq, bank(q), gt[:, 3:4], xq, ALU.mult, ALU.add).then_inc(s_end, 1)

        @block.tensor
        def _(pe):
            def turn(n, src, ready, base, free=None, banks=4, between=None):
                for q in range(4):
                    t, half = q % 2, q // 2
                    if between and q == 2:
                        between()
                    ready(half)
                    if free:
                        free(q)
                    for k in range(4):
                        last = pe.transpose(PS[:, base + q % banks, P * k:P * k + P], src(4 * half + k, t), ident)
                    last.then_inc(s_tp[n], 1)

            pe.wait_ge(s_in["cst"], 16)
            turn(0, lambda b, t: XN[:, b, P * t:P * t + P], lambda half: pe.wait_ge(s_xn[0], 4 * half + 4), 0)
            turn(0, lambda b, t: CN[:, b, P * t:P * t + P], lambda half: pe.wait_ge(s_in["ctx" + str(half)], 16), 4)
            turn(0, lambda b, t: CR[:, b, t, :], lambda half: pe.wait_ge(s_rev, half + 1), 0,
                 lambda q: pe.wait_ge(s_tv[0], q + 1))
            pe.wait_ge(s_vc, 1)
            pe.wait_ge(s_ct, 4)
            for q in range(4):
                pe.matmul(bank(4 + q), hskip[:, :], XS[:, 2 * q:2 * q + 2, :].rearrange("c b l -> c (b l)"),
                          start=True, stop=True).then_inc(s_skip, 1)

            def convolve_head(a, i, u):
                h = GROUP * i + u
                pe.wait_ge(s_T[a][u], 16 * (i + 1))
                pe.wait_ge(s_kv[a], h + 1)
                if not isinstance(i, int) or u >= YDEEP[a]:
                    pe.wait_ge(s_z[a], h + 1 - YDEEP[a])
                y = YBANK[a][u]
                near, far = TW[:, u, 0:P], TW[:, u, P:2 * P]
                early, late = KV[:, u % 2, 0:B * PAIRS], KV[:, u % 2, B * PAIRS:2 * B * PAIRS]
                pe.matmul(bank(y), near, early, start=True, stop=True)
                pe.matmul(bank(y + 1), near, late, start=True, stop=False)
                pe.matmul(bank(y + 1), far, early, start=False, stop=True).then_inc(s_conv[a], 1)

            def convolve(a, done):
                for u in range(done, GROUP):
                    convolve_head(a, 0, u)
                with pe.Fori(1, H // GROUP) as i:
                    for u in range(GROUP):
                        convolve_head(a, i, u)

            def back(a):
                pe.wait_ge(s_red[a], H)
                for q in range(4):
                    for k in range(4):
                        b, t = 2 * q + k // 2, k % 2
                        last = pe.transpose(PS[:, 4 + q, P * k:P * k + P], OT[:, t * B + b, :], ident)
                    last.then_inc(s_back[a], 1)

            pe.wait_ge(s_crt, 4)
            convolve(0, 0)
            back(0)

            turn(1, lambda b, t: XN[:, b, P * t:P * t + P], lambda half: pe.wait_ge(s_xn[1], 4 * half + 4), 0)
            pe.wait_ge(s_tv[1], 4)
            pe.wait_ge(s_in["rw"], 16)
            for b in range(B):
                for k in range(LT):
                    last = pe.matmul(PS[:, 4, E0 * b:E0 * b + E0], VT[:, k * B + b, :], RW0[:, k, :], start=k == 0,
                                     stop=k == LT - 1)
            last.then_inc(s_lg, 1)

            def tokens(k, n):
                return VT[:, k * B + 4 * n:k * B + 4 * n + 4, :].rearrange("p b c -> p (b c)")

            def shared_up(n, f):
                for k in range(LT):
                    last = pe.matmul(bank(f), SGU0[:, k, P * f:P * f + P], tokens(k, n), start=k == 0,
                                     stop=k == LT - 1)
                return last

            def shared_down(n):
                for b in range(4):
                    for k in range(2):
                        last = pe.matmul(PS[:, 2 * n + b // 2, L * (b % 2):L * (b % 2) + L],
                                         HS[:, n, k, P * b:P * b + P], SDN0[:, k, :], start=k == 0, stop=k == 1)
                last.then_inc(s_shdn, 1)

            pe.wait_ge(s_in["sh0"], 32)
            shared_up(0, 0)
            pe.wait_ge(s_oh, 1)
            pe.wait_ge(s_rev, 3)
            pos = PS[:, 5, 0:B * E0]
            pe.matmul(pos, lessb[:, :], oh[:, :, :].rearrange("p b e -> p (b e)"), start=True, stop=True)
            for d in range(1, B):
                pe.matmul(PS[:, 5, E0 * d:B * E0], onesb[:, :], oh[:, 0:B - d, :].rearrange("p b e -> p (b e)"),
                          start=False, stop=True, skip_group_check=True)
            pe.matmul(PS[:, 5, B * E0:2 * B * E0], onesb[:, :], oh[:, :, :].rearrange("p b e -> p (b e)"), start=True,
                      stop=True).then_inc(s_pos, 1)
            shared_up(0, 1)
            shared_up(0, 2)
            shared_up(0, 3).then_inc(s_shgu, 1)
            pe.wait_ge(s_shh, 2)
            for f in range(3):
                shared_up(1, f)
            shared_up(1, 3).then_inc(s_shgu, 1)

            def turn_block(j, par, first, loads):
                pe.wait_ge(s_xb[par], 16 * loads)
                if not first:
                    pe.wait_ge(s_bxt, j - 1)
                for k in range(LT):
                    last = pe.transpose(PS[:, par, P * k:P * k + P], XB[:, par, P * k:P * k + P], ident)
                last.then_inc(s_bx, 1)

            held = [pe.alloc_register(name=f"expert{par}") for par in range(2)]

            def read_expert(j, par):
                pe.reg_load(held[par], blki[0:1, j:j + 1] if isinstance(j, int) else blki[0:1, bass.ds(j, 1)])

            def expert(par):
                return pe.snap(held[par], min_val=0, max_val=E0 - 1)

            def up_block(j, par, e, first):
                pe.wait_ge(s_bxt, j + 1)
                if not first:
                    pe.wait_ge(s_bh, j - 1)
                for k in range(LT):
                    last = pe.matmul(bank(4 + par), XBT[:, par, k, :],
                                     GU0[:, bass.ds(e, 1), k, :].rearrange("p o f -> p (o f)"), start=k == 0,
                                     stop=k == LT - 1)
                last.then_inc(s_bgu, 1)

            def turn_hidden(j, par, first):
                pe.wait_ge(s_bh, j + 1)
                if not first:
                    pe.wait_ge(s_bht, j - 1)
                for k in range(F0 // P):
                    last = pe.transpose(PS[:, 2 + par, P * k:P * k + P], HB[:, par, P * k:P * k + P], ident)
                last.then_inc(s_bhp, 1)

            def down_block(j, par, e, first):
                pe.wait_ge(s_bht, j + 1)
                if not first:
                    pe.wait_ge(s_by, j - 1)
                for k in range(F0 // P):
                    last = pe.matmul(PS[:, 6 + par, 0:L], HBT[:, par, k, :],
                                     DN0[:, bass.ds(e, 1), k, :].rearrange("p o f -> p (o f)"), start=k == 0,
                                     stop=k == F0 // P - 1)
                last.then_inc(s_bdn, 1)

            pe.wait_ge(s_slot, 2)
            pe.wait_ge(s_w0[0], 16 * E0)
            pe.wait_ge(s_w0[1], 16 * E0)
            pe.wait_ge(s_shh, 4)

            def step(j, u, first, loads):
                turn_hidden(j, u, first)
                if not isinstance(j, int) or j + 1 < BLOCKS:
                    up_block(j + 1, 1 - u, expert(1 - u), first and u == 0)
                if not isinstance(j, int) or j + 2 < BLOCKS:
                    turn_block(j + 2, u, False, loads)
                down_block(j, u, expert(u), first)
                if not isinstance(j, int) or j + 2 < BLOCKS:
                    read_expert(j + 2, u)

            turn_block(0, 0, True, 1)
            read_expert(0, 0)
            up_block(0, 0, expert(0), True)
            read_expert(1, 1)
            turn_block(1, 1, True, 1)
            for u in range(2):
                step(u, u, True, 2)
            with pe.Fori(1, BLOCKS // 2 - 1) as i:
                for u in range(2):
                    step(2 * i + u, u, False, i + 2)
            for j in range(BLOCKS - 3, BLOCKS):
                step(j, j % 2, False, j // 2 + 2)

            pe.wait_ge(s_bht, BLOCKS)
            for n in range(2):
                shared_down(n)

            pe.wait_ge(s_by, BLOCKS)
            pe.wait_ge(s_shadd, 4)
            for u in range(EARLY - 1):
                convolve_head(1, 0, u)

            def two_banks(q):
                if q >= 2:
                    pe.wait_ge(s_tv[2], q - 1)

            turn(2, lambda b, t: XN[:, b, P * t:P * t + P], lambda half: pe.wait_ge(s_xn[2], 4 * half + 4), 0,
                 two_banks, 2, lambda: convolve_head(1, 0, EARLY - 1))
            pe.wait_ge(s_tv[2], 4)
            convolve(1, EARLY)
            back(1)

            turn(3, lambda b, t: XN[:, b, P * t:P * t + P], lambda half: pe.wait_ge(s_xn[3], 4 * half + 4), 0)
            pe.wait_ge(s_tv[3], 4)
            pe.wait_ge(s_in["rw1"], 16)
            for b in range(B):
                for k in range(LT):
                    last = pe.matmul(PS[:, 4 + b // 4, R1 * (b % 4):R1 * (b % 4) + R1], VT[:, k * B + b, :],
                                     RW1[:, k, :], start=k == 0, stop=k == LT - 1)
                if b % 4 == 3:
                    last.then_inc(s_lg1, 1)

            def split_product(dst, high, low, xh, xl, start, stop):
                pe.matmul(dst, high, xh, start=start, stop=False)
                pe.matmul(dst, high, xl, start=False, stop=False)
                return pe.matmul(dst, low, xh, start=False, stop=stop)

            def tok_half(t, k, n):
                return t[:, k * B + 4 * n:k * B + 4 * n + 4, :].rearrange("p b c -> p (b c)")

            pe.wait_ge(s_wsl, 1)
            pe.wait_ge(s_x1, 4)
            for n in range(NT):
                for k in range(LT):
                    w = slice(P * k, P * k + P)
                    last = split_product(bank(6 + n), WSH[:, w], WSL[:, w], tok_half(XH, k, n), tok_half(XL, k, n),
                                         k == 0, k == LT - 1)
                last.then_inc(s_sgu, 1)

            def up(p, u, n, first):
                if n == 0:
                    pe.wait_ge(s_wl[0], p + 1)
                if not first:
                    pe.wait_ge(s_mul, 2 * p + n - 1)
                for g in range(2):
                    for k in range(LT):
                        w = slice(P * (2 * k + g), P * (2 * k + g) + P)
                        last = split_product(bank(2 * n + g), WH[:, u, w], WL[:, u, w], tok_half(XH, k, n),
                                             tok_half(XL, k, n), k == 0, k == LT - 1)
                last.then_inc(s_gu, 1)

            def down(p, u, n, stop=False):
                pe.wait_ge(s_wl[1], p + 1)
                pe.wait_ge(s_lo, 2 * p + n + 1)
                for t in range(LT):
                    w = slice(2 * LT * P + P * t, 2 * LT * P + P * t + P)
                    last = split_product(bank(4 + 2 * t + n), WH[:, u, w], WL[:, u, w], HI[:, n, :], LO[:, n, :],
                                         False, stop)
                last.then_inc(s_dn, 1)

            up(0, 0, 0, True)
            pe.wait_ge(s_w1, 2)
            for b in range(B):
                last = pe.transpose(PS[0:R1, 4 + b // 4, P * (b % 4):P * (b % 4) + P], W1[:, b, :], ident)
                if b % 4 == 3:
                    last.then_inc(s_wt, 1)
            up(0, 0, 1, True)
            for n in range(NT):
                up(1, 1, n, False)
            pe.wait_ge(s_wts, 2)
            pe.wait_ge(s_ssi, 4)
            for n in range(NT):
                pe.wait_ge(s_slo, n + 1)
                for t in range(LT):
                    w = slice(LT * P + P * t, LT * P + P * t + P)
                    last = split_product(bank(4 + 2 * t + n), WSH[:, w], WSL[:, w], HI[:, n, :], LO[:, n, :],
                                         True, False)
                last.then_inc(s_sdn, 1)

            def pair(p, u):
                for n in range(NT):
                    up(p, u, n, False)
                    down(p - 1, 1 - u, n)

            for n in range(NT):
                down(0, 0, n)
            with pe.Fori(1, NP1 // 2) as i:
                for u in range(2):
                    pair(2 * i + u, u)
            for n in range(NT):
                down(NP1 - 1, 1, n, True)
            for q in range(4):
                for t in range(LT):
                    pe.wait_ge(s_acc[t], q // 2 + 1)
                for k in range(4):
                    b, t = 2 * q + k // 2, k % 2
                    last = pe.transpose(PS[:, q, P * k:P * k + P], OT[:, t * B + b, :], ident)
                last.then_inc(s_fin, 1)


INS = ["x", "ctx", "gates", "skip", "kp0", "kp1", "d1", "rw0", "gu0", "dn0", "sgu0", "sdn0", "rw1", "w1", "ws1", "cst"]


def kernel(**inputs):
    import numpy as np
    import concourse.bacc as bacc
    from concourse.bass_utils import run_bass_kernel_spmd

    a = {k: np.asarray(v) for k, v in inputs.items()}

    def padded(k):
        return np.concatenate([np.zeros((H, PAD), k.dtype), k, np.zeros((H, KP - PAD - L), k.dtype)], 1)

    gu1 = a["L1_ffn_gu_w"].reshape(NP1, 2, 2, I1, LT, P).transpose(0, 5, 4, 2, 1, 3).reshape(NP1, P, 2 * LT * P)
    dn1 = a["L1_ffn_dp_w"].reshape(NP1, 2, L, I1).transpose(0, 1, 3, 2).reshape(NP1, P, L)
    sgu1 = np.concatenate([a["L1_ffn_sh_gate_w"], a["L1_ffn_sh_up_w"]], 0).reshape(P, LT, P).transpose(2, 1, 0)
    sdn1 = np.concatenate([a["L1_ffn_sh_down_w"].T, np.zeros((P - I1, L), np.float32)], 0)
    arrays = {
        "x": a["x"],
        "ctx": a["ctx_2048"],
        "gates": np.stack([a["g_xattn"], a["g_ffn"]], 1).reshape(4),
        "skip": a["fside_S2_0"].reshape(P, 1),
        "kp0": padded(a["L0_xattn_k"]),
        "kp1": padded(a["L1_xattn_ssm_kernel"]),
        "d1": a["L1_xattn_D"].reshape(H, 1),
        "rw0": a["L0_ffn_router_w"],
        "gu0": np.concatenate([a["L0_ffn_gate_w"], a["L0_ffn_up_w"]], 2),
        "dn0": a["L0_ffn_down_w"],
        "sgu0": np.concatenate([a["L0_ffn_shared_gate_w"], a["L0_ffn_shared_up_w"]], 1),
        "sdn0": a["L0_ffn_shared_down_w"],
        "rw1": np.concatenate([a["L1_ffn_gate_w"], a["L1_ffn_sh_gate1_w"]], 0).T,
        "w1": np.concatenate([gu1, dn1], 2),
        "ws1": np.concatenate([sgu1.reshape(P, LT * P), sdn1], 1),
        "cst": shape_constants(),
    }
    nc = bacc.Bacc("TRN2", target_bir_lowering=False, num_devices=1)
    args = []
    for name in INS:
        arrays[name] = np.ascontiguousarray(arrays[name])
        args.append(nc.dram_tensor(name, arrays[name].shape, mybir.dt.from_np(arrays[name].dtype),
                                   kind="ExternalInput").ap())
    args.append(nc.dram_tensor("out", (B, C, L), F32, kind="ExternalOutput").ap())
    gated_layers(nc, *args)
    r = run_bass_kernel_spmd(nc, [arrays], core_ids=[0])
    return r.results[0]["out"]
```

```python
from contextlib import ExitStack

import concourse.bass as bass
from concourse import mybir

P = 128
B, C, L = 8, 128, 256
LT = L // P
HEAD = 8
H = C // HEAD
PAIRS = HEAD * HEAD
PAD = P - 1
KP = 384
E0, F0 = 8, 256
BLOCKS = B * C // P + E0 - 1
SLOTS = BLOCKS * P
E1, I1 = 64, 64
NP1 = E1 // 2
R1 = E1 + 1
GROUP = 4
YBANK = ((0, 2, 0, 2), (2, 4, 6, 0))
YDEEP = (2, 4)
EARLY = 3
SBANK = ((0, 1, 2, 3), (4, 6, 7, 5))
DBANK = (2, 3, 0, 1)
WARM_START, WARM_V, WARM_BACK, WARM_FFN, WARM_TURN, WARM_Q = 14, 2, 16, 14, (4, 2, 0), 8
TOK = B * C
NT = TOK // 512
WCOLS = LT * 2 * P + L
WPARTS = (slice(0, LT * 2 * P), slice(LT * 2 * P, WCOLS))
EPS = 1e-5

F32 = mybir.dt.float32
F32R = mybir.dt.float32r
BF16 = mybir.dt.bfloat16
I32 = mybir.dt.int32
ALU = mybir.AluOpType
ACT = mybir.ActivationFunctionType
AX = mybir.AxisListType

K_ID, K_LESS, K_HEAD = 0, P, 2 * P
K_FIRST = 3 * P
K_FULL = K_FIRST + E0
K_UPTO = K_FULL + E0 * E0
K_BLOCK = K_UPTO + E0 * E0
K_COLS = K_BLOCK + E0 * BLOCKS


def shape_constants():
    import numpy as np
    k = np.zeros((P, K_COLS), np.float32)
    a = np.arange(P)
    k[:, K_ID:K_ID + P] = np.eye(P)
    k[:, K_LESS:K_LESS + P] = a[:, None] < a[None, :]
    k[:, K_HEAD:K_HEAD + P] = a[:, None] // HEAD == a[None, :] // HEAD
    e = np.arange(E0)
    k[:, K_FIRST:K_FIRST + E0] = E0 - e
    k[:, K_FULL:K_FULL + E0 * E0] = np.tile(P * e, E0)
    k[:, K_UPTO:K_UPTO + E0 * E0] = (e[None, :] <= e[:, None]).reshape(-1)
    k[:, K_BLOCK:K_BLOCK + E0 * BLOCKS] = np.repeat(np.arange(BLOCKS), E0)
    return k


def gated_layers(nc, x, ctx_in, gates, skip, kp0, kp1, d1, rw0, gu0, dn0, sgu0, sdn0, rw1, w1, ws1, cst,
                 out):
    st = ExitStack()
    with st:
        def sb(name, shape, dt=F32):
            return st.enter_context(nc.sbuf_tensor(name, shape, dt))

        def sem(name):
            return st.enter_context(nc.semaphore(name))

        ffn0 = ExitStack()

        def sb0(name, shape, dt=F32):
            return ffn0.enter_context(nc.sbuf_tensor(name, shape, dt))

        kp1d = nc.dram_tensor("kp1d", [H, KP], F32, kind="Internal").ap()
        xsort = nc.dram_tensor("xsort", [SLOTS, L], F32, kind="Internal").ap()
        ysort = nc.dram_tensor("ysort", [SLOTS, L], F32, kind="Internal").ap()
        wtok = nc.dram_tensor("wtok", [R1, TOK], F32, kind="Internal").ap()

        X = sb("X", [P, B, L])
        CN = sb("CN", [P, B, L])
        XN = sb("XN", [P, B, L])
        XS = sb("XS", [P, B, L])
        CT = sb("CT", [P, LT * B, C])
        CRT = sb("CRT", [P, LT * B, C])
        VT = sb("VT", [P, LT * B, C])
        OT = sb("OT", [P, LT * B, C])
        TW = sb("TW", [P, 4, L])
        KV = sb("KV", [P, GROUP, LT * B * PAIRS])
        CR = KV[:, GROUP - 2:GROUP, :].rearrange("p u n -> p (u n)").rearrange("p (b t m) -> p b t m", b=B, t=LT)
        Z = sb("Z", [P, GROUP, LT * B * PAIRS])
        K = sb("K", [P, K_COLS])
        lessb = sb("lessb", [P, P], BF16)
        onesb = sb("onesb", [P, 512], BF16)
        skipc = sb("skipc", [P, 1])
        hskip = sb("hskip", [P, P])
        gt = sb("gt", [P, 4])
        gin = sb("gin", [P, 4])
        kpt = sb("kpt", [H, KP])
        dt1 = sb("dt1", [H, 1])
        neghalf = sb("neghalf", [P, B])
        stt = sb("stt", [P, B, 6])
        mv = sb("mv", [P, B, 2])
        ve = sb("ve", [P, B])
        negmean = sb("negmean", [P, B])
        shift = sb("shift", [P, B])
        rstd = sb("rstd", [P, B])
        LR = sb("LR", [R1, TOK])
        RW1 = sb("RW1", [P, LT, R1])
        WS = sb("WS", [P, LT * P + L])
        WR = sb("WR", [P, 2, WCOLS])
        RW0 = sb0("RW0", [P, LT, E0])
        GU0 = sb0("GU0", [P, E0, LT, 2 * F0])
        DN0 = sb0("DN0", [P, E0, F0 // P, L])
        SGU0 = sb0("SGU0", [P, LT, 2 * F0])
        SDN0 = sb0("SDN0", [P, F0 // P, L])
        HS = sb0("HS", [P, NT, 2, 512])
        LG = sb0("LG", [P, B, E0])
        eqm = sb0("eqm", [P, B, E0])
        mx = sb0("mx", [P, B])
        pick = sb0("pick", [P, B])
        oh = sb0("oh", [P, B, E0], BF16)
        ex = sb0("ex", [P, B])
        score = sb0("score", [P, B])
        cmpk = sb0("cmpk", [P, E0, E0])
        cnt = sb0("cnt", [P, E0])
        nblk = sb0("nblk", [P, E0])
        upto = sb0("upto", [P, E0])
        start0 = sb0("start0", [P, E0])
        blke = sb0("blke", [1, BLOCKS, E0])
        blkf = sb0("blkf", [1, BLOCKS])
        blki = sb0("blki", [1, BLOCKS], I32)
        slotm = sb0("slotm", [P, B, E0])
        slotf = sb0("slotf", [P, B])
        sloti = sb0("sloti", [P, B], I32)
        zero = sb0("zero", [P, L])
        XB = sb0("XB", [P, 2, L])
        XBT = sb0("XBT", [P, 2, LT, P])
        SG = sb0("SG", [P, 2, F0])
        HB = sb0("HB", [P, 2, F0])
        HBT = sb0("HBT", [P, 2, F0 // P, P])
        YB = sb0("YB", [P, 2, L])

        ffn0.close()
        XH = sb("XH", [P, LT * B, C], F32R)
        XL = sb("XL", [P, LT * B, C], F32R)
        WSH = sb("WSH", [P, LT * P + L], F32R)
        WSL = sb("WSL", [P, LT * P + L], F32R)
        WH = sb("WH", [P, 2, WCOLS], F32R)
        WL = sb("WL", [P, 2, WCOLS], F32R)
        WB = sb("WB", [P, 2, TOK])
        WBS = sb("WBS", [I1, TOK])
        SHS = sb("SHS", [I1, NT, 512])
        SHU = sb("SHU", [I1, NT, 512])
        SI = sb("SI", [P, 2, NT, 512])
        TK = sb("TK", [P, NT, 512])
        HI = sb("HI", [P, NT, 512], F32R)
        LO = sb("LO", [P, NT, 512], F32R)
        LG1 = sb("LG1", [P, B, R1])
        top = sb("top", [P, B, 8])
        rest = sb("rest", [P, B, E1])
        keep = sb("keep", [P, B, E1])
        ex1 = sb("ex1", [P, B, E1])
        exs = sb("exs", [P, B])
        den = sb("den", [P, B])
        rden = sb("rden", [P, B])
        W1 = sb("W1", [P, B, R1])
        WTS = sb("WTS", [R1, TOK])

        PS = st.enter_context(nc.psum_tensor("PS", [P, 8, 512], F32))
        ident = K[:, K_ID:K_ID + P]

        s_in = {n: sem("in_" + n) for n in ("x0", "x1", "ctx0", "ctx1", "cst", "small", "kp1", "kp1d", "rw", "sh0", "zero", "rw1", "ws1", "wtok", "wbs",
                                           "out")}
        s_w0 = [sem(f"in_w0_{e}") for e in range(2)]
        s_T = [[sem(f"in_toeplitz{a}_{u}") for u in range(4)] for a in range(2)]
        s_const = sem("constants_made")
        s_d1 = sem("d_added")
        s_dve = sem("vector_steps")
        s_gates = sem("gates_ready")
        s_var = [sem(f"variance{n}") for n in range(4)]
        s_ve = [sem(f"variance_plus_eps{n}") for n in range(4)]
        s_rstd = [sem(f"rstd{n}") for n in range(4)]
        s_xn = [sem(f"normed{n}") for n in range(4)]
        s_rev = [sem(f"ctx_reversed{n}") for n in range(2)]
        s_less = sem("less_mask")
        s_tp0 = sem("turned_in_psum0")
        s_tp = [s_tp0] + [sem(f"turned_in_psum{n}") for n in (1, 2, 3)]
        s_tv = [sem(f"turned{n}") for n in range(4)]
        s_ct = sem("ctx_turned")
        s_crt = sem("reversed_ctx_turned")
        s_vc = sem("v_times_ctx")
        s_skip = sem("skip_sums")
        s_skc = sem("skip_times_ctx")
        s_kv = [sem(f"kv{a}") for a in range(2)]
        s_conv = [sem(f"conv{a}") for a in range(2)]
        s_z = [sem(f"times_query{a}") for a in range(2)]
        s_red = [sem(f"summed{a}") for a in range(2)]
        s_back = [sem(f"back_in_psum{a}") for a in range(2)]
        s_res = [sem(f"residual{a}") for a in range(2)]
        s_lg = sem("logits0")
        s_mx = sem("best_logit")
        s_ex = sem("exp_best")
        s_oh = sem("onehot")
        s_pos = sem("positions")
        s_slot = sem("slots")
        s_xs = sem("scaled_tokens")
        s_scat = sem("scattered")
        s_shgu = sem("shared_gu")
        s_shsi = sem("shared_silu")
        s_shh = sem("shared_hidden")
        s_shdn = sem("shared_down")
        s_shadd = sem("shared_added")
        s_bx = sem("block_turned_psum")
        s_bxt = sem("block_turned")
        s_bgu = sem("block_gu")
        s_bsi = sem("block_silu")
        s_bh = sem("block_hidden")
        s_bhp = sem("block_hidden_psum")
        s_bht = sem("block_hidden_turned")
        s_bdn = sem("block_down")
        s_by = sem("block_y")
        s_byo = [sem(f"block_stored{i}") for i in range(2)]
        s_xb = [sem(f"in_block{i}") for i in range(2)]
        s_yg = [sem(f"gathered{b}") for b in range(B)]
        s_raw = [sem(f"in_raw{i}") for i in range(2)]
        s_wb = [sem(f"in_weights_of_tokens{i}") for i in range(2)]
        s_xh = sem("x_high")
        s_x1 = sem("x_split")
        s_lt = [sem(f"logits_rows{n}") for n in range(2)]
        s_lte = [sem(f"logits_rows_out{n}") for n in range(2)]
        s_lg1 = sem("logits1")
        s_lgr = sem("logits1_out")
        s_e1 = sem("exp_in")
        s_ee = sem("exp_out")
        s_w1 = sem("token_weights")
        s_wt = sem("token_weights_psum")
        s_wts = sem("token_weights_turned")
        s_wsh = sem("shared1_high")
        s_wsl = sem("shared1_low")
        s_sgu = sem("shared1_gu")
        s_ssi = sem("shared1_silu")
        s_stw = sem("shared1_weighted")
        s_shi = sem("shared1_hi")
        s_slo = sem("shared1_lo")
        s_sdn = sem("shared1_down")
        s_wh = [sem("pair_high_up"), sem("pair_high_down")]
        s_wl = [sem("pair_low_up"), sem("pair_low_down")]
        s_gu = sem("pair_gu")
        s_si = sem("pair_silu")
        s_mul = sem("pair_product")
        s_tw = sem("pair_weighted")
        s_hi = sem("pair_hi")
        s_lo = sem("pair_lo")
        s_dn = sem("pair_down")
        s_acc = [sem(f"sum_out_of_psum{t}") for t in range(LT)]
        s_fin = sem("final_psum")
        s_end = sem("final")
        block = st.enter_context(nc.Block())

        x_n = x.rearrange("b c l -> c b l")
        c_n = ctx_in.rearrange("b c l -> c b l")
        out_n = out.rearrange("b c l -> c b l")

        def bank(i, n=512):
            return PS[:, i, 0:n]

        def two(q):
            return slice(2 * q, 2 * q + 2)

        def turned_in(i):
            return bank(i).rearrange("p (b t c) -> p b t c", b=2, t=LT)

        def turned_out(dst, q):
            return dst[:, :, :].rearrange("p (t b) c -> p b t c", t=LT)[:, two(q), :, :]

        def head(t, h):
            return t[:, :, bass.ds(HEAD * h, HEAD)]

        def over_j(ap):
            return ap.unsqueeze(3).broadcast_to([P, LT * B, HEAD, HEAD])

        def over_i(ap):
            return ap.unsqueeze(2).broadcast_to([P, LT * B, HEAD, HEAD])

        def pairs(ap):
            return ap.rearrange("p (a i j) -> p a i j", i=HEAD, j=HEAD)

        @block.sync
        def _(sp):
            for name, dst, src in (("x", X, x_n), ("ctx", CN, c_n)):
                for half in range(2):
                    b = slice(4 * half, 4 * half + 4)
                    sp.dma_start(dst[:, b, :], src[:, b, :]).then_inc(s_in[name + str(half)], 16)

            def toeplitz(a, kp, h, u):
                rows = bass.AP(tensor=kp.tensor, offset=0, ap=[[KP, H], [1, P], [1, L]])
                sp.dma_start(TW[:, u:u + 1, :], rows[bass.ds(h, 1), :, :].rearrange("o p l -> p o l")
                             ).then_inc(s_T[a][u], 16)

            for a, kp in ((0, kp0), (1, kp1d)):
                if a:
                    sp.wait_ge(s_in["kp1d"], 16)
                for u in range(4):
                    if a:
                        sp.wait_ge(s_conv[0], H)
                    toeplitz(a, kp, u, u)
                with sp.Fori(1, H // GROUP) as i:
                    for u in range(4):
                        sp.wait_ge(s_conv[a], GROUP * i + (u - 3))
                        toeplitz(a, kp, GROUP * i + u, u)
                if a == 0:
                    sp.wait_ge(s_scat, 16 * B)
                    xs_r = xsort.rearrange("(j p) l -> p j l", p=P)

                    def load_x(j, par):
                        sp.dma_start(XB[:, par:par + 1, :], xs_r[:, bass.ds(j, 1), :]).then_inc(s_xb[par], 16)

                    def step(j, par):
                        sp.wait_ge(s_bx, j + 1)
                        load_x(j + 2, par)

                    load_x(0, 0)
                    load_x(1, 1)
                    with sp.Fori(0, BLOCKS // 2 - 1) as i:
                        for par in range(2):
                            step(2 * i + par, par)
                    step(BLOCKS - 3, 0)

            def raw(p, u):
                sp.dma_start(WR[:, u:u + 1, :], w1[bass.ds(p, 1), :, :].rearrange("o p n -> p o n")
                             ).then_inc(s_raw[u], 16)

            def token_weights(p, u):
                rows = bass.AP(tensor=wtok.tensor, offset=0, ap=[[TOK, R1], [0, I1], [1, TOK]])
                for e in range(2):
                    sp.dma_start(WB[I1 * e:I1 * e + I1, u:u + 1, :],
                                 rows[bass.ds(2 * p + e, 1), :, :].rearrange("o p t -> p o t")
                                 ).then_inc(s_wb[u], 16)

            def raw_again(p, u):
                for part in range(2):
                    sp.wait_ge(s_wl[part], p - 1)
                raw(p, u)

            def token_weights_again(p, u):
                sp.wait_ge(s_tw, 2 * p - 2)
                token_weights(p, u)

            for u in range(2):
                raw(u, u)
            for u in range(2):
                raw_again(2 + u, u)
            sp.wait_ge(s_in["wtok"], 16)
            sp.dma_start(WBS[:, :], wtok[E1:E1 + 1, :].partition_broadcast(I1)).then_inc(s_in["wbs"], 16)
            for u in range(2):
                token_weights(u, u)
            with sp.Fori(1, NP1 // 2 - 1) as i:
                for u in range(2):
                    token_weights_again(2 * i + u, u)
                    raw_again(2 * i + 2 + u, u)
            for u in range(2):
                token_weights_again(NP1 - 2 + u, u)
            for q in range(4):
                sp.wait_ge(s_end, q + 1)
                sp.dma_start(out_n[:, 2 * q:2 * q + 2, :], X[:, 2 * q:2 * q + 2, :]).then_inc(s_in["out"], 16)
            sp.wait_ge(s_in["out"], 64)

        @block.gpsimd
        def _(pool):
            pool.memset(onesb[:], 1.0).then_inc(s_const, 1)
            pool.memset(neghalf[:], -0.5).then_inc(s_const, 1)
            pool.memset(zero[:], 0.0).then_inc(s_const, 1)

            def rstd_of(n):
                for q in range(4):
                    b = two(q)
                    pool.wait_ge(s_const, 2)
                    pool.wait_ge(s_var[n], 2 * q + 2)
                    if n:
                        pool.wait_ge(s_xn[n - 1], B)
                    pool.tensor_scalar_add(ve[:, b], mv[:, b, 1], EPS).then_inc(s_ve[n], 1)
                    pool.tensor_scalar(negmean[:, b], mv[:, b, 0], -1.0, None, ALU.mult).then_inc(s_ve[n], 1)
                    pool.wait_ge(s_ve[n], 2 * q + 2)
                    pool.tensor_tensor(rstd[:, b], ve[:, b], neghalf[:, b], ALU.pow).then_inc(s_rstd[n], 1)
                    pool.wait_ge(s_rstd[n], 2 * q + 1)
                    pool.tensor_tensor(shift[:, b], negmean[:, b], rstd[:, b], ALU.mult).then_inc(s_rstd[n], 1)

            def product(a, left, right, h, u, first):
                if not first:
                    pool.wait_ge(s_conv[a], h + 1 - GROUP)
                pool.tensor_tensor(pairs(KV[:, u, :]), over_j(head(left, h)), over_i(head(right, h)),
                                   ALU.mult).then_inc(s_kv[a], 1)

            def products(a, left, right, done):
                for u in range(done, GROUP):
                    product(a, left, right, u, u, True)
                with pool.Fori(1, H // GROUP) as i:
                    for u in range(GROUP):
                        product(a, left, right, GROUP * i + u, u, False)

            rstd_of(0)
            pool.wait_ge(s_tv[0], 4)
            pool.wait_ge(s_crt, 4)
            for u in range(2):
                product(0, VT, CRT, u, u, True)
            pool.wait_ge(s_skc, 4)
            products(0, VT, CRT, 2)
            rstd_of(1)
            pool.wait_ge(s_slot, 1)
            pool.wait_ge(s_in["zero"], 16)
            for b in range(B):
                pool.wait_ge(s_xs, b + 1)
                pool.indirect_dma_start(out=xsort, out_offset=bass.IndirectOffsetOnAxis(ap=sloti[:, b:b + 1], axis=0),
                                        in_=XS[:, b, :], in_offset=None).then_inc(s_scat, 16)
            pool.wait_ge(s_conv[0], H)
            for u in range(EARLY):
                product(1, CRT, CRT, u, u, True)
            ys_r = ysort.rearrange("(j p) l -> p j l", p=P)

            def store_y(j, par):
                pool.wait_ge(s_by, j + 1)
                pool.dma_start(ys_r[:, bass.ds(j, 1), :], YB[:, par:par + 1, :]).then_inc(s_byo[par], 16)

            with pool.Fori(0, BLOCKS // 2) as i:
                for par in range(2):
                    store_y(2 * i + par, par)
            store_y(BLOCKS - 1, 0)
            pool.wait_ge(s_byo[0], 16 * ((BLOCKS + 1) // 2))
            pool.wait_ge(s_byo[1], 16 * (BLOCKS // 2))
            pool.wait_ge(s_scat, 16 * B)
            for b in range(B):
                pool.indirect_dma_start(out=XS[:, b, :], out_offset=None, in_=ysort,
                                        in_offset=bass.IndirectOffsetOnAxis(ap=sloti[:, b:b + 1], axis=0)
                                        ).then_inc(s_yg[b], 16)
            rstd_of(2)
            products(1, CRT, CRT, EARLY)
            pool.wait_ge(s_wsh, 1)
            pool.tensor_tensor(WSL[:, :], WS[:, :], WSH[:, :].bitcast(F32), ALU.subtract).then_inc(s_wsl, 1)

            def low(p, u):
                for part in range(2):
                    pool.wait_ge(s_wh[part], p + 1)
                    w = WPARTS[part]
                    pool.tensor_tensor(WL[:, u, w], WR[:, u, w], WH[:, u, w].bitcast(F32), ALU.subtract
                                       ).then_inc(s_wl[part], 1)

            for u in range(2):
                low(u, u)
            rstd_of(3)
            for q in range(4):
                pool.wait_ge(s_xh, q + 1)
                pool.tensor_tensor(turned_out(XL, q), turned_out(VT, q), turned_out(XH, q).bitcast(F32), ALU.subtract
                                   ).then_inc(s_x1, 1)
            with pool.Fori(1, NP1 // 2) as i:
                for u in range(2):
                    low(2 * i + u, u)

        @block.scalar
        def _(act):
            act.dma_start(K[:, :], cst).then_inc(s_in["cst"], 16)
            act.dma_start(gin[:, :], gates.partition_broadcast(P)).then_inc(s_in["small"], 16)
            act.dma_start(skipc[:, :], skip).then_inc(s_in["small"], 16)
            act.dma_start(kpt[:, :], kp1).then_inc(s_in["kp1"], 16)
            act.dma_start(dt1[:, :], d1).then_inc(s_in["kp1"], 16)

            def normed_quarter(n, dst, q):
                act.wait_ge(s_rstd[n], 2 * q + 2)
                for b in range(2 * q, 2 * q + 2):
                    act.activation(dst(b), X[:, b, :].rearrange("c (t m) -> c t m", t=LT), ACT.Identity,
                                   scale=rstd[:, b:b + 1], bias=shift[:, b:b + 1]).then_inc(s_xn[n], 1)

            def normed(n, dst):
                for q in range(4):
                    normed_quarter(n, dst, q)

            def forward(b):
                return XN[:, b, :].rearrange("c (t m) -> c t m", t=LT)

            normed(0, lambda b: forward(b)[:, :, ::-1])
            act.wait_ge(s_in["ctx0"], 16)
            act.activation(CR[:, 0:4, :, :], CN[:, 0:4, :].rearrange("c b (t m) -> c b t m", t=LT)[:, :, :, ::-1],
                           ACT.Copy).then_inc(s_rev[0], 1)

            def out_of_psum(n, dst, q, first, bnk, done):
                act.wait_ge(s_tp[n], first + q + 1)
                act.activation(turned_out(dst, q), turned_in(bnk), ACT.Copy).then_inc(done, 1)

            def logits_out(n, q, rows):
                act.wait_ge(s_lt[n], q + 1)
                act.activation(LR[0:rows, L * q:L * q + L], PS[0:rows, 4 + q, 0:L], ACT.Copy).then_inc(s_lte[n], 1)

            def normed_and_turned(n, banks=4, logits=None):
                for q in range(4):
                    normed_quarter(n, forward, q)
                    if q:
                        out_of_psum(n, VT, q - 1, 0, (q - 1) % banks, s_tv[n])
                if logits:
                    logits(0)
                    logits(1)
                out_of_psum(n, VT, 3, 0, 3 % banks, s_tv[n])
                if logits:
                    logits(2)
                    logits(3)

            for q in range(4):
                out_of_psum(0, CT, q, q + 1, 4 + q, s_ct)
            for q in range(4):
                out_of_psum(0, CRT, q, 8, q, s_crt)
            act.wait_ge(s_in["cst"], 16)
            act.activation(lessb[:, :], K[:, K_LESS:K_LESS + P], ACT.Copy).then_inc(s_less, 1)
            act.wait_ge(s_in["small"], 32)
            act.activation(gt[:, :], gin[:, :], ACT.Tanh).then_inc(s_gates, 1)
            act.dma_start(RW0[:, :, :], rw0.rearrange("(k p) e -> p k e", p=P)).then_inc(s_in["rw"], 16)
            act.dma_start(SGU0[:, :, :], sgu0.rearrange("(k p) f -> p k f", p=P)).then_inc(s_in["sh0"], 16)
            act.dma_start(SDN0[:, :, :], sdn0.rearrange("(k p) f -> p k f", p=P)).then_inc(s_in["sh0"], 16)
            act.wait_ge(s_const, 3)
            act.dma_start(xsort.rearrange("(j p) l -> p j l", p=P),
                          zero[:].unsqueeze(1).broadcast_to([P, BLOCKS, L])).then_inc(s_in["zero"], 16)
            for e in range(E0):
                act.wait_ge(s_conv[0], e + 1)
                act.dma_start(GU0[:, e, :, :], gu0[e].rearrange("(k p) f -> p k f", p=P)).then_inc(s_w0[0], 16)
                act.dma_start(DN0[:, e, :, :], dn0[e].rearrange("(k p) f -> p k f", p=P)).then_inc(s_w0[1], 16)
            act.wait_ge(s_d1, 1)
            act.dma_start(kp1d, kpt[:, :]).then_inc(s_in["kp1d"], 16)
            act.dma_start(RW1[:, :, :], rw1.rearrange("(k p) e -> p k e", p=P)).then_inc(s_in["rw1"], 16)
            act.dma_start(WS[:, :], ws1).then_inc(s_in["ws1"], 16)
            act.wait_ge(s_kv[0], H)
            normed_and_turned(1, logits=lambda q: logits_out(0, q, E0))
            act.wait_ge(s_mx, 1)
            act.activation(ex[:, :], mx[:, :], ACT.Exp, scale=-1.0).then_inc(s_ex, 1)
            for n in range(2):
                act.wait_ge(s_shgu, n + 1)
                for f in range(2):
                    act.activation(HS[:, n, f, :], bank(SBANK[n][f]), ACT.Silu).then_inc(s_shsi, 1)

            def turn_block(j, par, first):
                act.wait_ge(s_bx, j + 1)
                if not first:
                    act.wait_ge(s_bgu, j - 1)
                act.activation(XBT[:, par, :, :], PS[:, par, 0:L].rearrange("p (k s) -> p k s", k=LT), ACT.Copy
                               ).then_inc(s_bxt, 1)

            def silu_block(j, par, first):
                act.wait_ge(s_bgu, j + 1)
                if not first:
                    act.wait_ge(s_bh, j - 1)
                act.activation(SG[:, par, :], PS[:, 4 + par, 0:F0], ACT.Silu).then_inc(s_bsi, 1)

            def block_out(j, u, stored):
                act.wait_ge(s_bdn, j + 1)
                if stored is not None:
                    act.wait_ge(s_byo[u], stored)
                act.activation(YB[:, u, :], PS[:, 6 + u, 0:L], ACT.Copy).then_inc(s_by, 1)

            turn_block(0, 0, True)
            turn_block(1, 1, True)
            silu_block(0, 0, True)
            silu_block(1, 1, True)
            turn_block(2, 0, False)
            for j in range(2):
                silu_block(j + 2, j, False)
                turn_block(j + 3, 1 - j, False)
                block_out(j, j, None)
            with act.Fori(1, (BLOCKS - 3) // 2) as i:
                for u in range(2):
                    silu_block(2 * i + u + 2, u, False)
                    turn_block(2 * i + u + 3, 1 - u, False)
                    block_out(2 * i + u, u, 16 * i)
            for j in range(BLOCKS - 3, BLOCKS):
                if j + 2 < BLOCKS:
                    silu_block(j + 2, j % 2, False)
                block_out(j, j % 2, 16 * (j // 2))

            normed_and_turned(2, 2)


            def high(part, p, u, first):
                act.wait_ge(s_raw[u], 16 * (p // 2 + 1) if isinstance(p, int) else first)
                if not isinstance(p, int) or p >= 2:
                    act.wait_ge((s_gu, s_dn)[part], 2 * p - 2)
                w = WPARTS[part]
                act.activation(WH[:, u, w], WR[:, u, w], ACT.Copy).then_inc(s_wh[part], 1)

            act.wait_ge(s_in["ws1"], 16)
            act.activation(WSH[:, :], WS[:, :], ACT.Copy).then_inc(s_wsh, 1)
            for p in range(2):
                for part in range(2):
                    high(part, p, p, None)
            act.wait_ge(s_z[1], H)
            normed_and_turned(3, logits=lambda q: logits_out(1, q, R1))
            for n in range(2):
                b = slice(4 * n, 4 * n + 4)
                act.wait_ge(s_e1, n + 1)
                act.activation(ex1[:, b, :], ex1[:, b, :], ACT.Exp).then_inc(s_ee, 1)
                act.activation(exs[:, b], LG1[:, b, E1], ACT.Exp, scale=-1.0).then_inc(s_ee, 1)
            for n in range(NT):
                act.wait_ge(s_sgu, n + 1)
                act.activation(SHS[:, n, :], PS[0:I1, 4 + n, :], ACT.Silu).then_inc(s_ssi, 1)
                act.activation(SHU[:, n, :], PS[I1:P, 4 + n, :], ACT.Copy).then_inc(s_ssi, 1)

            def silu(p, u, n):
                act.wait_ge(s_gu, 2 * p + n + 1)
                if not isinstance(p, int) or p >= 2:
                    act.wait_ge(s_tw, 2 * p + n - 3)
                act.activation(SI[:, u, n, :], bank(2 * n), ACT.Silu).then_inc(s_si, 1)

            def hidden_high(p, n, first):
                act.wait_ge(s_tw, 2 * p + n + 1)
                if not first:
                    act.wait_ge(s_dn, 2 * p + n - 1)
                act.activation(HI[:, n, :], TK[:, n, :], ACT.Copy).then_inc(s_hi, 1)

            silu(0, 0, 0)
            for n in range(2):
                act.wait_ge(s_wt, n + 1)
                act.activation(WTS[:, 512 * n:512 * n + 512], PS[0:R1, 6 + n, :], ACT.Copy).then_inc(s_wts, 1)
            act.wait_ge(s_wts, 2)
            act.dma_start(wtok, WTS[:, :]).then_inc(s_in["wtok"], 16)
            silu(0, 0, 1)
            silu(1, 1, 0)
            high(0, 2, 0, None)
            for n in range(NT):
                act.wait_ge(s_stw, n + 1)
                act.activation(LO[0:I1, n, :], SHU[:, n, :], ACT.Copy).then_inc(s_shi, 1)
            silu(1, 1, 1)
            for n in range(NT):
                hidden_high(0, n, True)
            hidden_high(1, 0, False)
            high(1, 2, 0, None)
            hidden_high(1, 1, False)

            def pair(p, u, more, nxt):
                for n in range(NT):
                    silu(p, u, n)
                    if n == 0 and more:
                        high(0, p + 1, 1 - u, nxt)
                    hidden_high(p, n, False)
                    if n == 1 and more:
                        high(1, p + 1, 1 - u, nxt)

            with act.Fori(1, NP1 // 2 - 1) as i:
                pair(2 * i, 0, True, 16 * (i + 1))
                pair(2 * i + 1, 1, True, 16 * (i + 2))
            pair(NP1 - 2, 0, True, None)
            pair(NP1 - 1, 1, False, None)
            for n in range(NT):
                act.wait_ge(s_dn, 2 * NP1 - 1 + n)
                act.activation(OT[:, 4 * n:4 * n + 4, :].rearrange("p b c -> p (b c)"), bank(4 + n), ACT.Copy
                               ).then_inc(s_acc[0], 1)

        @block.vector
        def _(dve):
            n_own = [0]

            def own(ins):
                n_own[0] += 1
                ins.then_inc(s_dve, 1)

            def settle():
                if n_own[0]:
                    dve.wait_ge(s_dve, n_own[0])

            def norm_stats(n, before):
                if n:
                    dve.wait_ge(s_rstd[n - 1], 8)
                for q in range(4):
                    before(q)
                    settle()
                    for b in range(2 * q, 2 * q + 2):
                        own(dve.bn_stats(stt[:, b, :], X[:, b, :]))
                    settle()
                    for b in range(2 * q, 2 * q + 2):
                        dve.bn_aggr(mv[:, b, :], stt[:, b, :]).then_inc(s_var[n], 1)

            def v_out_of_psum(quarters):
                for q in quarters:
                    dve.wait_ge(s_tp[0], 2 * q + 1)
                    dve.tensor_copy(turned_out(VT, q), turned_in(q)).then_inc(s_tv[0], 1)

            norm_stats(0, lambda q: dve.wait_ge(s_in["x" + str(q // 2)], 16))
            v_out_of_psum((0, 1))
            dve.wait_ge(s_in["ctx1"], 16)
            dve.tensor_copy(CR[:, 4:8, :, :], CN[:, 4:8, :].rearrange("c b (t m) -> c b t m", t=LT)[:, :, :, ::-1]
                            ).then_inc(s_rev[1], 1)
            v_out_of_psum((2, 3))
            dve.wait_ge(s_xn[0], B)
            CRf = CR.rearrange("c b t m -> c b (t m)")
            for half in range(2):
                b = slice(4 * half, 4 * half + 4)
                dve.wait_ge(s_rev[half], 1)
                dve.tensor_tensor(XS[:, b, :], XN[:, b, :], CRf[:, b, :], ALU.mult).then_inc(s_vc, 1)
            dve.wait_ge(s_in["cst"], 16)
            dve.wait_ge(s_in["small"], 32)
            dve.tensor_scalar(hskip[:, :], K[:, K_HEAD:K_HEAD + P], skipc[:, 0:1], None, ALU.mult).then_inc(s_vc, 1)
            dve.wait_ge(s_in["kp1"], 32)
            dve.tensor_tensor(kpt[:, PAD:PAD + 1], kpt[:, PAD:PAD + 1], dt1[:, :], ALU.add).then_inc(s_d1, 1)
            dve.wait_ge(s_gates, 1)
            for q in range(4):
                b = slice(2 * q, 2 * q + 2)
                dve.wait_ge(s_skip, q + 1)
                dve.tensor_tensor(XS[:, b, :], bank(4 + q).rearrange("c (b l) -> c b l", b=2), CRf[:, b, :],
                                  ALU.mult).then_inc(s_skc, 1)
            dve.wait_ge(s_skc, 4)
            for b in range(B):
                own(dve.scalar_tensor_tensor(
                    X[:, b, :].rearrange("c (t m) -> c t m", t=LT),
                    XS[:, b, :].rearrange("c (t m) -> c t m", t=LT)[:, :, ::-1], gt[:, 0:1],
                    X[:, b, :].rearrange("c (t m) -> c t m", t=LT), ALU.mult, ALU.add))

            def combine(a, query):
                def times_query(h, u, first):
                    dve.wait_ge(s_conv[a], h + 1)
                    if not first:
                        dve.wait_ge(s_red[a], h + 1 - GROUP)
                    y = PS[:, YBANK[a][u]:YBANK[a][u] + 2, :].rearrange("p t n -> p (t n)")
                    dve.tensor_tensor(pairs(Z[:, u, :]), pairs(y), over_j(head(query, h)), ALU.mult
                                      ).then_inc(s_z[a], 1)

                def sums(h, u):
                    dve.wait_ge(s_z[a], h + 1)
                    dve.tensor_reduce(head(OT, h), pairs(Z[:, u, :]).rearrange("p a i j -> p a j i"), AX.X,
                                      ALU.add).then_inc(s_red[a], 1)

                times_query(0, 0, True)
                times_query(1, 1, True)
                sums(0, 0)
                for u in range(2, GROUP):
                    times_query(u, u, True)
                    sums(u - 1, u - 1)
                with dve.Fori(1, H // GROUP - 1) as i:
                    for u in range(GROUP):
                        times_query(GROUP * i + u, u, False)
                        sums(GROUP * i + u - 1, (u - 1) % GROUP)
                for h in range(H - GROUP, H - 1):
                    times_query(h, h % GROUP, False)
                    sums(h - 1, (h - 1) % GROUP)
                sums(H - 2, (H - 2) % GROUP)
                times_query(H - 1, (H - 1) % GROUP, False)
                sums(H - 1, (H - 1) % GROUP)

            def add_back(a, g, q):
                xq = X[:, two(q), :].rearrange("c b l -> c (b l)")
                dve.wait_ge(s_back[a], q + 1)
                own(dve.scalar_tensor_tensor(xq, bank(4 + q), g, xq, ALU.mult, ALU.add))

            dve.wait_ge(s_ct, 4)
            settle()
            combine(0, CT)

            norm_stats(1, lambda q: add_back(0, gt[:, 0:1], q))
            dve.wait_ge(s_lg, 1)
            own(dve.tensor_copy(LG[:, :, :], PS[:, 0, 0:B * E0].rearrange("p (b e) -> p b e", b=B)))
            settle()
            dve.tensor_reduce(mx[:, :], LG[:, :, :], AX.X, ALU.max).then_inc(s_mx, 1)
            dve.wait_ge(s_mx, 1)
            own(dve.tensor_tensor(eqm[:, :, :], LG[:, :, :], mx[:].unsqueeze(2).broadcast_to([P, B, E0]),
                                  ALU.is_equal))
            settle()
            own(dve.tensor_tensor(LG[:, :, :], eqm[:, :, :],
                                  K[:, K_FIRST:K_FIRST + E0].unsqueeze(1).broadcast_to([P, B, E0]), ALU.mult))
            settle()
            own(dve.tensor_reduce(pick[:, :], LG[:, :, :], AX.X, ALU.max))
            settle()
            dve.tensor_tensor(oh[:, :, :], LG[:, :, :], pick[:].unsqueeze(2).broadcast_to([P, B, E0]),
                              ALU.is_equal).then_inc(s_oh, 1)
            dve.wait_ge(s_ex, 1)
            own(dve.tensor_scalar_add(ex[:, :], ex[:, :], 1.0))
            settle()
            own(dve.reciprocal(score[:, :], ex[:, :]))
            settle()
            dve.wait_ge(s_pos, 1)
            own(dve.tensor_reduce(cnt[:, :], PS[:, 5, B * E0:2 * B * E0].rearrange("p (b e) -> p e b", b=B), AX.X,
                                  ALU.add))
            settle()
            own(dve.tensor_tensor(cmpk[:, :, :], cnt[:].unsqueeze(2).broadcast_to([P, E0, E0]),
                                  K[:, K_FULL:K_FULL + E0 * E0].rearrange("p (e k) -> p e k", e=E0), ALU.is_gt))
            settle()
            own(dve.tensor_reduce(nblk[:, :], cmpk[:, :, :], AX.X, ALU.add))
            settle()
            own(dve.tensor_tensor(cmpk[:, :, :], nblk[:].unsqueeze(1).broadcast_to([P, E0, E0]),
                                  K[:, K_UPTO:K_UPTO + E0 * E0].rearrange("p (e k) -> p e k", e=E0), ALU.mult))
            settle()
            own(dve.tensor_reduce(upto[:, :], cmpk[:, :, :], AX.X, ALU.add))
            settle()
            own(dve.tensor_tensor(start0[:, :], upto[:, :], nblk[:, :], ALU.subtract))
            settle()
            own(dve.tensor_scalar(start0[:, :], start0[:, :], float(P), None, ALU.mult))
            settle()
            own(dve.tensor_tensor(slotm[:, :, :], PS[:, 5, 0:B * E0].rearrange("p (b e) -> p b e", b=B),
                                  start0[:].unsqueeze(1).broadcast_to([P, B, E0]), ALU.add))
            settle()
            own(dve.tensor_tensor(slotm[:, :, :], slotm[:, :, :], oh[:, :, :], ALU.mult))
            settle()
            own(dve.tensor_reduce(slotf[:, :], slotm[:, :, :], AX.X, ALU.add))
            settle()
            dve.tensor_copy(sloti[:, :], slotf[:, :]).then_inc(s_slot, 1)
            dve.wait_ge(s_xn[1], B)
            for b in range(B):
                dve.tensor_scalar(XS[:, b, :], XN[:, b, :], score[:, b:b + 1], None, ALU.mult).then_inc(s_xs, 1)
            own(dve.tensor_tensor(blke[:, :, :], upto[0:1, :].unsqueeze(1).broadcast_to([1, BLOCKS, E0]),
                                  K[0:1, K_BLOCK:K_BLOCK + E0 * BLOCKS].rearrange("p (j e) -> p j e", e=E0),
                                  ALU.is_le))
            settle()
            own(dve.tensor_reduce(blkf[:, :], blke[:, :, :], AX.X, ALU.add))
            settle()
            own(dve.tensor_scalar_min(blkf[:, :], blkf[:, :], float(E0 - 1)))
            settle()
            dve.tensor_copy(blki[:, :], blkf[:, :]).then_inc(s_slot, 1)
            for n in range(2):
                for f in range(2):
                    dve.wait_ge(s_shsi, 2 * n + f + 1)
                    dve.tensor_tensor(HS[:, n, f, :], HS[:, n, f, :], bank(SBANK[n][2 + f]), ALU.mult
                                      ).then_inc(s_shh, 1)

            def add_shared(q):
                dve.wait_ge(s_shdn, q // 2 + 1)
                xq = X[:, two(q), :].rearrange("c b l -> c (b l)")
                dve.scalar_tensor_tensor(xq, bank(DBANK[q]), gt[:, 1:2], xq, ALU.mult, ALU.add).then_inc(s_shadd, 1)

            for q in range(2):
                add_shared(q)

            def hidden(j, u, first):
                dve.wait_ge(s_bsi, j + 1)
                if not first:
                    dve.wait_ge(s_bhp, j - 1)
                dve.tensor_tensor(HB[:, u, :], SG[:, u, :], PS[:, 4 + u, F0:2 * F0], ALU.mult).then_inc(s_bh, 1)

            def hidden_turned(j, u, first):
                dve.wait_ge(s_bhp, j + 1)
                if not first:
                    dve.wait_ge(s_bdn, j - 1)
                dve.tensor_copy(HBT[:, u, :, :], PS[:, 2 + u, 0:F0].rearrange("p (k s) -> p k s", k=F0 // P)
                                ).then_inc(s_bht, 1)

            hidden(0, 0, True)
            hidden(1, 1, True)
            hidden_turned(0, 0, True)
            for j in range(2):
                hidden(j + 2, j, False)
                hidden_turned(j + 1, 1 - j, j == 0)
            with dve.Fori(1, BLOCKS // 2 - 1) as i:
                for u in range(2):
                    hidden(2 * i + u + 2, u, False)
                    hidden_turned(2 * i + u + 1, 1 - u, False)
            hidden(BLOCKS - 1, (BLOCKS - 1) % 2, False)
            for j in range(BLOCKS - 2, BLOCKS):
                hidden_turned(j, j % 2, False)
            for q in range(2, 4):
                add_shared(q)

            def gathered(q):
                dve.wait_ge(s_shadd, 4)
                for b in range(2 * q, 2 * q + 2):
                    dve.wait_ge(s_yg[b], 16)
                    own(dve.scalar_tensor_tensor(X[:, b, :], XS[:, b, :], gt[:, 1:2], X[:, b, :], ALU.mult, ALU.add))

            norm_stats(2, gathered)
            dve.wait_ge(s_tv[2], 4)
            dve.wait_ge(s_red[0], H)
            combine(1, VT)

            norm_stats(3, lambda q: add_back(1, gt[:, 2:3], q))

            def high_x(q):
                dve.wait_ge(s_tv[3], q + 1)
                dve.tensor_copy(turned_out(XH, q), turned_out(VT, q)).then_inc(s_xh, 1)

            def best(n):
                b = slice(4 * n, 4 * n + 4)
                dve.wait_ge(s_lg1, n + 1)
                dve.tensor_copy(LG1[:, b, :], PS[:, n, 0:4 * R1].rearrange("p (b e) -> p b e", b=4)
                                ).then_inc(s_lgr, 1)
                dve.wait_ge(s_lgr, n + 1)
                for i in range(4 * n, 4 * n + 4):
                    own(dve.max(top[:, i, :], LG1[:, i, 0:E1]))
                settle()
                dve.tensor_tensor(ex1[:, b, :], LG1[:, b, 0:E1], top[:, b, 0:1].broadcast_to([P, 4, E1]),
                                  ALU.subtract).then_inc(s_e1, 1)
                for i in range(4 * n, 4 * n + 4):
                    own(dve.match_replace(rest[:, i, :], top[:, i, :], LG1[:, i, 0:E1], -3.0e38))
                settle()
                own(dve.tensor_tensor(keep[:, b, :], rest[:, b, :], LG1[:, b, 0:E1], ALU.not_equal))
                settle()

            def softmax(n):
                b = slice(4 * n, 4 * n + 4)
                dve.wait_ge(s_ee, 2 * n + 2)
                own(dve.tensor_tensor(keep[:, b, :], keep[:, b, :], ex1[:, b, :], ALU.mult))
                own(dve.tensor_scalar_add(exs[:, b], exs[:, b], 1.0))
                settle()
                own(dve.tensor_reduce(den[:, b], keep[:, b, :], AX.X, ALU.add))
                settle()
                own(dve.reciprocal(rden[:, b], den[:, b]))
                dve.reciprocal(W1[:, b, E1], exs[:, b]).then_inc(s_w1, 1)
                settle()
                dve.tensor_tensor(W1[:, b, 0:E1], keep[:, b, :], rden[:, b].unsqueeze(2).broadcast_to([P, 4, E1]),
                                  ALU.mult).then_inc(s_w1, 1)

            for q in range(4):
                high_x(q)
            for n in range(2):
                best(n)
            for n in range(2):
                softmax(n)

            def product(p, u, n):
                dve.wait_ge(s_si, 2 * p + n + 1)
                dve.tensor_tensor(SI[:, u, n, :], SI[:, u, n, :], bank(2 * n + 1), ALU.mult).then_inc(s_mul, 1)

            def weighted(p, u, n, rounds):
                dve.wait_ge(s_wb[u], 32 * rounds)
                dve.wait_ge(s_mul, 2 * p + n + 1)
                dve.tensor_tensor(TK[:, n, :], SI[:, u, n, :], WB[:, u, 512 * n:512 * n + 512], ALU.mult
                                  ).then_inc(s_tw, 1)

            def hidden_low(p, n):
                dve.wait_ge(s_hi, 2 * p + n + 1)
                dve.tensor_tensor(LO[:, n, :], TK[:, n, :], HI[:, n, :].bitcast(F32), ALU.subtract
                                  ).then_inc(s_lo, 1)

            for n in range(NT):
                dve.wait_ge(s_ssi, 2 * n + 2)
                own(dve.tensor_tensor(SHU[:, n, :], SHS[:, n, :], SHU[:, n, :], ALU.mult))
            for n in range(NT):
                product(0, 0, n)
            product(1, 1, 0)
            settle()
            dve.wait_ge(s_in["wbs"], 16)
            for n in range(NT):
                dve.tensor_tensor(SHU[:, n, :], SHU[:, n, :], WBS[:, 512 * n:512 * n + 512], ALU.mult
                                  ).then_inc(s_stw, 1)
            for n in range(NT):
                dve.wait_ge(s_shi, n + 1)
                dve.tensor_tensor(LO[I1:P, n, :], SHU[:, n, :], LO[0:I1, n, :].bitcast(F32), ALU.subtract
                                  ).then_inc(s_slo, 1)
            for n in range(NT):
                weighted(0, 0, n, 1)
            for n in range(NT):
                dve.wait_ge(s_sdn, n + 1)
                hidden_low(0, n)
            for n in range(NT):
                if n:
                    product(1, 1, n)
                dve.wait_ge(s_lo, n + 1)
                weighted(1, 1, n, 1)
                hidden_low(1, n)

            with dve.Fori(1, NP1 // 2) as i:
                for u in range(2):
                    for n in range(NT):
                        product(2 * i + u, u, n)
                        weighted(2 * i + u, u, n, i + 1)
                        hidden_low(2 * i + u, n)
            for n in range(NT):
                dve.wait_ge(s_dn, 2 * NP1 - 1 + n)
                dve.tensor_copy(OT[:, B + 4 * n:B + 4 * n + 4, :].rearrange("p b c -> p (b c)"), bank(6 + n)
                                ).then_inc(s_acc[1], 1)
            for q in range(4):
                dve.wait_ge(s_fin, q + 1)
                xq = X[:, 2 * q:2 * q + 2, :].rearrange("c b l -> c (b l)")
                dve.scalar_tensor_tensor(xq, bank(q), gt[:, 3:4], xq, ALU.mult, ALU.add).then_inc(s_end, 1)

        @block.tensor
        def _(pe):
            def turn_quarter(n, src, q, bnk):
                for k in range(4):
                    last = pe.transpose(PS[:, bnk, P * k:P * k + P], src(2 * q + k // LT, k % LT), ident)
                last.then_inc(s_tp[n], 1)

            def keep_warm(bnk, count):
                for _ in range(count):
                    pe.matmul(bank(bnk), onesb[:, 0:P], onesb[:, :], start=True, stop=True)

            def half_of(t):
                return lambda b, k: t[:, b, P * k:P * k + P]

            def turn_normed(n, q, banks=4):
                pe.wait_ge(s_xn[n], 2 * q + 2)
                turn_quarter(n, half_of(XN), q, q % banks)

            pe.wait_ge(s_const, 1)
            keep_warm(0, WARM_START)
            pe.wait_ge(s_in["cst"], 16)
            for q in range(4):
                turn_normed(0, q)
                if q < 3:
                    keep_warm(7, WARM_V)
                pe.wait_ge(s_in["ctx" + str(q // 2)], 16)
                turn_quarter(0, half_of(CN), q, 4 + q)
            for q in range(4):
                pe.wait_ge(s_rev[q // 2], 1)
                pe.wait_ge(s_tv[0], q + 1)
                turn_quarter(0, lambda b, t: CR[:, b, t, :], q, q)

            def turn_and_route(n, rw, rows, row, done):
                def route(q):
                    pe.wait_ge(s_tv[2 * n + 1], q + 1)
                    for k in range(LT):
                        last = pe.matmul(PS[0:rows, 4 + q, 0:L], rw[:, k, :],
                                         VT[:, k * B + 2 * q:k * B + 2 * q + 2, :].rearrange("p b c -> p (b c)"),
                                         start=k == 0, stop=k == LT - 1)
                    last.then_inc(s_lt[n], 1)

                def turn_logits(q):
                    pe.wait_ge(s_lte[n], q + 1)
                    for b in range(2 * q, 2 * q + 2):
                        last = pe.transpose(row(b), LR[0:rows, P * b:P * b + P], ident[0:rows, 0:rows])
                    if (q + 1) % (4 // done) == 0:
                        last.then_inc((s_lg, s_lg1)[n], 1)

                keep_warm(3, WARM_FFN)
                for q in range(4):
                    turn_normed(2 * n + 1, q)
                    if q < 3:
                        keep_warm(3, WARM_TURN[q])
                    if q:
                        route(q - 1)
                for q in range(2):
                    turn_logits(q)
                route(3)
                for q in range(2, 4):
                    turn_logits(q)

            pe.wait_ge(s_vc, 3)
            pe.wait_ge(s_ct, 4)
            for q in range(4):
                pe.matmul(bank(4 + q), hskip[:, :], XS[:, 2 * q:2 * q + 2, :].rearrange("c b l -> c (b l)"),
                          start=True, stop=True).then_inc(s_skip, 1)

            def convolve_head(a, i, u):
                h = GROUP * i + u
                pe.wait_ge(s_T[a][u], 16 * (i + 1))
                pe.wait_ge(s_kv[a], h + 1)
                if not isinstance(i, int) or u >= YDEEP[a]:
                    pe.wait_ge(s_z[a], h + 1 - YDEEP[a])
                y = YBANK[a][u]
                near, far = TW[:, u, 0:P], TW[:, u, P:2 * P]
                early, late = KV[:, u, 0:B * PAIRS], KV[:, u, B * PAIRS:2 * B * PAIRS]
                pe.matmul(bank(y), near, early, start=True, stop=True)
                pe.matmul(bank(y + 1), near, late, start=True, stop=False)
                pe.matmul(bank(y + 1), far, early, start=False, stop=True).then_inc(s_conv[a], 1)

            def convolve(a, done):
                for u in range(done, GROUP):
                    convolve_head(a, 0, u)
                with pe.Fori(1, H // GROUP) as i:
                    for u in range(GROUP):
                        convolve_head(a, i, u)

            def back(a):
                if a:
                    pe.wait_ge(s_z[a], H - 2)
                keep_warm(4, WARM_BACK)
                pe.wait_ge(s_red[a], H)
                for q in range(4):
                    for k in range(4):
                        b, t = 2 * q + k // 2, k % 2
                        last = pe.transpose(PS[:, 4 + q, P * k:P * k + P], OT[:, t * B + b, :], ident)
                    last.then_inc(s_back[a], 1)

            pe.wait_ge(s_crt, 4)
            convolve(0, 0)
            back(0)

            pe.wait_ge(s_in["rw"], 16)
            turn_and_route(0, RW0, E0, lambda b: PS[:, 0, E0 * b:E0 * b + E0], 1)

            def tokens(k, n):
                return VT[:, k * B + 4 * n:k * B + 4 * n + 4, :].rearrange("p b c -> p (b c)")

            def shared_up(n, f):
                for k in range(LT):
                    last = pe.matmul(bank(SBANK[n][f]), SGU0[:, k, P * f:P * f + P], tokens(k, n), start=k == 0,
                                     stop=k == LT - 1)
                return last

            def shared_down(n):
                for b in range(4):
                    for k in range(2):
                        last = pe.matmul(PS[:, DBANK[2 * n + b // 2], L * (b % 2):L * (b % 2) + L],
                                         HS[:, n, k, P * b:P * b + P], SDN0[:, k, :], start=k == 0, stop=k == 1)
                last.then_inc(s_shdn, 1)

            pe.wait_ge(s_in["sh0"], 32)
            shared_up(0, 1)
            pe.wait_ge(s_oh, 1)
            pe.wait_ge(s_less, 1)
            pos = PS[:, 5, 0:B * E0]
            pe.matmul(pos, lessb[:, :], oh[:, :, :].rearrange("p b e -> p (b e)"), start=True, stop=True)
            for d in range(1, B):
                pe.matmul(PS[:, 5, E0 * d:B * E0], onesb[:, 0:P], oh[:, 0:B - d, :].rearrange("p b e -> p (b e)"),
                          start=False, stop=True, skip_group_check=True)
            pe.matmul(PS[:, 5, B * E0:2 * B * E0], onesb[:, 0:P], oh[:, :, :].rearrange("p b e -> p (b e)"), start=True,
                      stop=True).then_inc(s_pos, 1)
            shared_up(0, 0)
            shared_up(0, 2)
            shared_up(0, 3).then_inc(s_shgu, 1)
            for f in range(3):
                shared_up(1, f)
            pe.wait_ge(s_slot, 1)
            shared_up(1, 3).then_inc(s_shgu, 1)
            pe.wait_ge(s_shh, 2)
            shared_down(0)

            def turn_block(j, par, first, loads):
                pe.wait_ge(s_xb[par], 16 * loads)
                if not first:
                    pe.wait_ge(s_bxt, j - 1)
                for k in range(LT):
                    last = pe.transpose(PS[:, par, P * k:P * k + P], XB[:, par, P * k:P * k + P], ident)
                last.then_inc(s_bx, 1)

            held = [pe.alloc_register(name=f"expert{k}") for k in range(3)]

            def read_expert(j, k):
                pe.reg_load(held[k], blki[0:1, j:j + 1] if isinstance(j, int) else blki[0:1, bass.ds(j, 1)])

            def expert(k):
                return pe.snap(held[k], min_val=0, max_val=E0 - 1)

            def next_expert(j):
                for k in range(2):
                    pe.reg_mov(held[k], held[k + 1])
                read_expert(j, 2)

            def up_block(j, par, e, first):
                pe.wait_ge(s_bxt, j + 1)
                if not first:
                    pe.wait_ge(s_bh, j - 1)
                for k in range(LT):
                    last = pe.matmul(bank(4 + par), XBT[:, par, k, :],
                                     GU0[:, bass.ds(e, 1), k, :].rearrange("p o f -> p (o f)"), start=k == 0,
                                     stop=k == LT - 1)
                last.then_inc(s_bgu, 1)

            def turn_hidden(j, par, first):
                pe.wait_ge(s_bh, j + 1)
                if not first:
                    pe.wait_ge(s_bht, j - 1)
                for k in range(F0 // P):
                    last = pe.transpose(PS[:, 2 + par, P * k:P * k + P], HB[:, par, P * k:P * k + P], ident)
                last.then_inc(s_bhp, 1)

            def down_block(j, par, e, first):
                pe.wait_ge(s_bht, j + 1)
                if not first:
                    pe.wait_ge(s_by, j - 1)
                for k in range(F0 // P):
                    last = pe.matmul(PS[:, 6 + par, 0:L], HBT[:, par, k, :],
                                     DN0[:, bass.ds(e, 1), k, :].rearrange("p o f -> p (o f)"), start=k == 0,
                                     stop=k == F0 // P - 1)
                last.then_inc(s_bdn, 1)

            pe.wait_ge(s_slot, 2)
            pe.wait_ge(s_w0[0], 16 * E0)
            pe.wait_ge(s_w0[1], 16 * E0)
            pe.wait_ge(s_shh, 4)

            def step(j, u, loads):
                whole = not isinstance(j, int)
                if whole or j + 2 < BLOCKS:
                    up_block(j + 2, u, expert(2), not whole and j < 0)
                if whole or j + 1 < BLOCKS:
                    turn_hidden(j + 1, 1 - u, not whole and j < 1)
                if whole or j + 3 < BLOCKS:
                    turn_block(j + 3, 1 - u, False, loads)
                down_block(j, u, expert(0), not whole and j < 2)
                if whole or j + 3 < BLOCKS:
                    next_expert(j + 3)

            turn_block(0, 0, True, 1)
            turn_block(1, 1, True, 1)
            for k in range(2):
                read_expert(k, k)
                up_block(k, k, expert(k), True)
            read_expert(2, 2)
            turn_block(2, 0, False, 2)
            pe.wait_ge(s_shadd, 2)
            turn_hidden(0, 0, True)
            for u in range(2):
                step(u, u, u // 2 + 2 + u)
            with pe.Fori(1, (BLOCKS - 3) // 2) as i:
                for u in range(2):
                    step(2 * i + u, u, i + 2 + u)
            for j in range(BLOCKS - 3, BLOCKS):
                step(j, j % 2, 0)

            pe.wait_ge(s_bht, BLOCKS)
            pe.wait_ge(s_bxt, BLOCKS)
            shared_down(1)

            pe.wait_ge(s_by, BLOCKS)
            pe.wait_ge(s_shadd, 4)
            for u in range(EARLY):
                convolve_head(1, 0, u)

            for q in range(4):
                if q < 2:
                    keep_warm(1, WARM_Q)
                else:
                    pe.wait_ge(s_tv[2], q - 1)
                turn_normed(2, q, 2)
            pe.wait_ge(s_tv[2], 4)
            convolve(1, EARLY)
            back(1)

            pe.wait_ge(s_in["rw1"], 16)
            turn_and_route(1, RW1, R1, lambda b: PS[:, b // 4, R1 * (b % 4):R1 * (b % 4) + R1], 2)

            def split_product(dst, high, low, xh, xl, start, stop):
                pe.matmul(dst, high, xh, start=start, stop=False)
                pe.matmul(dst, high, xl, start=False, stop=False)
                return pe.matmul(dst, low, xh, start=False, stop=stop)

            def tok_half(t, k, n):
                return t[:, k * B + 4 * n:k * B + 4 * n + 4, :].rearrange("p b c -> p (b c)")

            pe.wait_ge(s_wsl, 1)
            pe.wait_ge(s_x1, 4)
            for n in range(NT):
                for k in range(LT):
                    w = slice(P * k, P * k + P)
                    last = split_product(bank(4 + n), WSH[:, w], WSL[:, w], tok_half(XH, k, n), tok_half(XL, k, n),
                                         k == 0, k == LT - 1)
                last.then_inc(s_sgu, 1)

            def up(p, u, n, first):
                if n == 0:
                    pe.wait_ge(s_wl[0], p + 1)
                if not first:
                    pe.wait_ge(s_mul, 2 * p + n - 1)
                for g in range(2):
                    for k in range(LT):
                        w = slice(P * (2 * k + g), P * (2 * k + g) + P)
                        last = split_product(bank(2 * n + g), WH[:, u, w], WL[:, u, w], tok_half(XH, k, n),
                                             tok_half(XL, k, n), k == 0, k == LT - 1)
                last.then_inc(s_gu, 1)

            def down(p, u, n, stop=False):
                pe.wait_ge(s_wl[1], p + 1)
                pe.wait_ge(s_lo, 2 * p + n + 1)
                for t in range(LT):
                    w = slice(2 * LT * P + P * t, 2 * LT * P + P * t + P)
                    last = split_product(bank(4 + 2 * t + n), WH[:, u, w], WL[:, u, w], HI[:, n, :], LO[:, n, :],
                                         False, stop)
                last.then_inc(s_dn, 1)

            pe.wait_ge(s_lgr, 2)
            up(0, 0, 0, True)
            for b in range(B):
                pe.wait_ge(s_w1, 2 * (b // 4) + 2)
                last = pe.transpose(PS[0:R1, 6 + b // 4, P * (b % 4):P * (b % 4) + P], W1[:, b, :], ident)
                if b % 4 == 3:
                    last.then_inc(s_wt, 1)
            up(0, 0, 1, True)
            for n in range(NT):
                up(1, 1, n, False)
            up(2, 0, 0, False)
            pe.wait_ge(s_wts, 2)
            pe.wait_ge(s_ssi, 4)
            for n in range(NT):
                pe.wait_ge(s_slo, n + 1)
                for t in range(LT):
                    w = slice(LT * P + P * t, LT * P + P * t + P)
                    pe.matmul(bank(4 + 2 * t + n), WSH[:, w], LO[:, n, :], start=True, stop=False)
                    last = pe.matmul(bank(4 + 2 * t + n), WSL[:, w], LO[:, n, :], start=False, stop=False)
                last.then_inc(s_sdn, 1)

            def pair(p, u, more=True):
                down(p - 1, 1 - u, 0)
                up(p, u, 1, False)
                down(p - 1, 1 - u, 1)
                if more:
                    up(p + 1, 1 - u, 0, False)

            for n in range(NT):
                down(0, 0, n)
            with pe.Fori(1, NP1 // 2 - 1) as i:
                for u in range(2):
                    pair(2 * i + u, u)
            pair(NP1 - 2, 0)
            pair(NP1 - 1, 1, False)
            for n in range(NT):
                down(NP1 - 1, 1, n, True)
            for q in range(4):
                for t in range(LT):
                    pe.wait_ge(s_acc[t], q // 2 + 1)
                for k in range(4):
                    b, t = 2 * q + k // 2, k % 2
                    last = pe.transpose(PS[:, q, P * k:P * k + P], OT[:, t * B + b, :], ident)
                last.then_inc(s_fin, 1)


INS = ["x", "ctx", "gates", "skip", "kp0", "kp1", "d1", "rw0", "gu0", "dn0", "sgu0", "sdn0", "rw1", "w1", "ws1", "cst"]


def kernel(**inputs):
    import numpy as np
    import concourse.bacc as bacc
    from concourse.bass_utils import run_bass_kernel_spmd

    a = {k: np.asarray(v) for k, v in inputs.items()}

    def padded(k):
        return np.concatenate([np.zeros((H, PAD), k.dtype), k, np.zeros((H, KP - PAD - L), k.dtype)], 1)

    gu1 = a["L1_ffn_gu_w"].reshape(NP1, 2, 2, I1, LT, P).transpose(0, 5, 4, 2, 1, 3).reshape(NP1, P, 2 * LT * P)
    dn1 = a["L1_ffn_dp_w"].reshape(NP1, 2, L, I1).transpose(0, 1, 3, 2).reshape(NP1, P, L)
    sgu1 = np.concatenate([a["L1_ffn_sh_gate_w"], a["L1_ffn_sh_up_w"]], 0).reshape(P, LT, P).transpose(2, 1, 0)
    sdn1 = np.concatenate([a["L1_ffn_sh_down_w"].T] * 2, 0)
    arrays = {
        "x": a["x"],
        "ctx": a["ctx_2048"],
        "gates": np.stack([a["g_xattn"], a["g_ffn"]], 1).reshape(4),
        "skip": a["fside_S2_0"].reshape(P, 1),
        "kp0": padded(a["L0_xattn_k"]),
        "kp1": padded(a["L1_xattn_ssm_kernel"]),
        "d1": a["L1_xattn_D"].reshape(H, 1),
        "rw0": a["L0_ffn_router_w"],
        "gu0": np.concatenate([a["L0_ffn_gate_w"], a["L0_ffn_up_w"]], 2),
        "dn0": a["L0_ffn_down_w"],
        "sgu0": np.concatenate([a["L0_ffn_shared_gate_w"], a["L0_ffn_shared_up_w"]], 1),
        "sdn0": a["L0_ffn_shared_down_w"],
        "rw1": np.concatenate([a["L1_ffn_gate_w"], a["L1_ffn_sh_gate1_w"]], 0).T,
        "w1": np.concatenate([gu1, dn1], 2),
        "ws1": np.concatenate([sgu1.reshape(P, LT * P), sdn1], 1),
        "cst": shape_constants(),
    }
    nc = bacc.Bacc("TRN2", target_bir_lowering=False, num_devices=1)
    args = []
    for name in INS:
        arrays[name] = np.ascontiguousarray(arrays[name])
        args.append(nc.dram_tensor(name, arrays[name].shape, mybir.dt.from_np(arrays[name].dtype),
                                   kind="ExternalInput").ap())
    args.append(nc.dram_tensor("out", (B, C, L), F32, kind="ExternalOutput").ap())
    gated_layers(nc, *args)
    r = run_bass_kernel_spmd(nc, [arrays], core_ids=[0])
    return r.results[0]["out"]
```
